# Optimizing a Trainium2 kernel written in Bass

```python
import numpy as np
import jax
import jax.numpy as jnp

def _softmax(x, axis=-1):
    return jax.nn.softmax(x, axis=axis)

def _gelu(x):
    return jax.nn.gelu(x, approximate=True)

def _silu(x):
    return jax.nn.silu(x)

def _sigmoid(x):
    return jax.nn.sigmoid(x)

def _layernorm(x, axis=-1, eps=1e-05):
    m = jnp.mean(x, axis=axis, keepdims=True)
    v = jnp.var(x, axis=axis, keepdims=True)
    return (x - m) / jnp.sqrt(v + eps)

def _scatter_add(tgt, idx, src, axis=0):
    return tgt.at[idx].add(src)

def _segment_sum(src, seg, n):
    return jax.ops.segment_sum(src, seg, n)
kernel_name = 'mk_sandwich_d1_jaxref_r8_5c4851'

def setup_inputs(seed: int=0):
    np.random.seed(seed)
    _w = jnp.asarray

    def _L0_attn_setup():
        import jax, jax.numpy as jnp
        import numpy as np
        B, L, IN_DIM = (4, 256, 128)
        H, D = (16, 64)
        OUT_DIM = 128
        key = jax.random.key(seed)
        k1, k2, k3 = jax.random.split(key, 3)
        inputs = jax.random.normal(k1, (B, L, IN_DIM), dtype=jnp.float32)
        W_qkv = jax.random.normal(k2, (IN_DIM, 3 * H * D), dtype=jnp.float32) * IN_DIM ** (-0.5)
        W_out = jax.random.normal(k3, (H * D, OUT_DIM), dtype=jnp.float32) * (H * D) ** (-0.5)
        return {'inputs': inputs, 'W_qkv': W_qkv, 'W_out': W_out}
    _L0_attn_in = _L0_attn_setup()

    def _L0_ffn_setup():
        import jax, jax.numpy as jnp
        import numpy as np
        D_MODEL = 128
        D_FF = 512
        N_EXPERTS = 8
        INIT_SCALE = 0.1

        def _trunc_normal(key, shape, std):
            return std * jax.random.truncated_normal(key, -2.0, 2.0, shape, dtype=jnp.float32)
        key = jax.random.key(seed)
        ks = jax.random.split(key, 5)
        x = jax.random.normal(ks[0], (4, 128, D_MODEL), dtype=jnp.float32)
        router_W = _trunc_normal(ks[1], (D_MODEL, N_EXPERTS), INIT_SCALE / np.sqrt(D_MODEL))
        router_b = jnp.zeros((N_EXPERTS,), dtype=jnp.float32)
        W1 = _trunc_normal(ks[2], (N_EXPERTS, D_MODEL, D_FF), INIT_SCALE / np.sqrt(D_MODEL))
        b1 = jnp.zeros((N_EXPERTS, D_FF), dtype=jnp.float32)
        W2 = _trunc_normal(ks[3], (N_EXPERTS, D_FF, D_MODEL), INIT_SCALE / np.sqrt(D_FF))
        b2 = jnp.zeros((N_EXPERTS, D_MODEL), dtype=jnp.float32)
        return {'x': x, 'router_W': router_W, 'router_b': router_b, 'W1': W1, 'b1': b1, 'W2': W2, 'b2': b2}
    _L0_ffn_in = _L0_ffn_setup()
    _d = {'L0_attn_inputs': _L0_attn_in['inputs'], 'L0_attn_W_qkv': _L0_attn_in['W_qkv'], 'L0_attn_W_out': _L0_attn_in['W_out'], 'L0_ffn_router_W': _L0_ffn_in['router_W'], 'L0_ffn_router_b': _L0_ffn_in['router_b'], 'L0_ffn_W1': _L0_ffn_in['W1'], 'L0_ffn_b1': _L0_ffn_in['b1'], 'L0_ffn_W2': _L0_ffn_in['W2'], 'L0_ffn_b2': _L0_ffn_in['b2']}
    _x0 = _d['L0_attn_inputs']
    _d['L0_attn_inputs'] = jax.random.normal(jax.random.fold_in(jax.random.key(seed), 1), (2, 1024, 128), dtype=_x0.dtype)
    del _x0
    return _d

def reference(L0_attn_inputs, L0_attn_W_qkv, L0_attn_W_out, L0_ffn_router_W, L0_ffn_router_b, L0_ffn_W1, L0_ffn_b1, L0_ffn_W2, L0_ffn_b2):

    def _L0_attn_ref(inputs, W_qkv, W_out):
        import jax, jax.numpy as jnp
        import numpy as np
        B, L, IN_DIM = (4, 256, 128)
        H, D = (16, 64)
        OUT_DIM = 128
        b, l, _ = inputs.shape
        qkv = inputs @ W_qkv
        q, k, v = jnp.split(qkv, 3, axis=-1)
        q = q.reshape(b, l, H, D)
        k = k.reshape(b, l, H, D)
        v = v.reshape(b, l, H, D)
        score = jnp.einsum('bihd,bjhd->bijh', q, k) / D ** 0.5
        mask = jnp.tril(jnp.ones((l, l), dtype=score.dtype))[None, :, :, None]
        masked_score = score * mask + 1e+30 * (mask - 1.0)
        wmat = jax.nn.softmax(masked_score, axis=2)
        out = jnp.einsum('bijh,bjhd->bihd', wmat, v).reshape(b, l, H * D)
        return out @ W_out

    def _L0_ffn_ref(x, router_W, router_b, W1, b1, W2, b2):
        import jax, jax.numpy as jnp
        import numpy as np
        D_MODEL = 128
        D_FF = 512
        N_EXPERTS = 8
        INIT_SCALE = 0.1

        def _trunc_normal(key, shape, std):
            return std * jax.random.truncated_normal(key, -2.0, 2.0, shape, dtype=jnp.float32)
        logits = jnp.einsum('bsd,de->bse', x.astype(jnp.float32), router_W) + router_b
        probs = jax.nn.softmax(logits, axis=-1)
        top1 = jnp.argmax(probs, axis=-1)
        mask = jax.nn.one_hot(top1, N_EXPERTS, dtype=x.dtype)
        gates = mask * probs.astype(x.dtype)
        h = jax.nn.relu(jnp.einsum('bsd,edf->besf', x, W1) + b1[:, None, :])
        y = jnp.einsum('besf,efd->besd', h, W2) + b2[:, None, :]
        out = jnp.einsum('bse,besd->bsd', gates, y)
        return out
    x = L0_attn_inputs
    x = x + _layernorm(_L0_attn_ref(_layernorm(x, axis=-1), L0_attn_W_qkv, L0_attn_W_out), axis=-1)
    x = x + _layernorm(_L0_ffn_ref(_layernorm(x, axis=-1), L0_ffn_router_W, L0_ffn_router_b, L0_ffn_W1, L0_ffn_b1, L0_ffn_W2, L0_ffn_b2), axis=-1)
    return x

_drawn_inputs = setup_inputs


def setup_inputs(seed=0):
    import zlib

    import numpy as np

    out = dict(_drawn_inputs(seed))
    spreads = {'L0_ffn_router_b': (0.0, 0.1), 'L0_ffn_b1': (0.0, 0.1), 'L0_ffn_b2': (0.0, 0.1)}
    factors = {}
    for name, (base, spread) in spreads.items():
        noise = np.random.default_rng([zlib.crc32(name.encode()), seed]).standard_normal(out[name].shape)
        drawn = base * np.exp(spread * noise) if base else spread * noise
        out[name] = jnp.asarray(drawn.astype(out[name].dtype))
    for name, factor in factors.items():
        out[name] = (out[name] * factor).astype(out[name].dtype)
    return out
```

```python
from contextlib import ExitStack

import concourse.bass as bass
from concourse import mybir

F32 = mybir.dt.float32
F32R = mybir.dt.float32r
BF16 = mybir.dt.bfloat16
F16 = mybir.dt.float16
ALU = mybir.AluOpType
ACT = mybir.ActivationFunctionType
AX_X = mybir.AxisListType.X

P = 128
EPS = 1e-5
NEG = -1.0e30


def step_order(r, first, last):
    o = [] if first and r == 0 else [("O", k) for k in range(4)]
    m = [] if last and r == 3 else [("M", i) for i in range(8)] + [("R", 0)]
    if r % 2 == 0:
        q = [] if last and r == 2 else [("Q", i) for i in range(4)]
        v, ty = [], []
    else:
        q = []
        v = [] if last else [("V", 0), ("V", 1)]
        if last and r == 1:
            v = [("V", 0), ("V", 1)]
        ty = [] if first and r == 1 else [("T", 0), ("Y", 0), ("T", 1), ("Y", 1)]
    s = [("S", j) for j in range(8)]

    def take(l, n=1):
        out = l[:n]
        del l[:n]
        return out

    order = []
    order += take(m) + take(s) + take(m) + take(s) + take(o) + take(m) + take(ty) + take(m) + take(s)
    order += take(o) + take(ty) + take(m) + take(s) + take(m) + take(ty) + take(s) + take(m) + take(s)
    order += take(o) + take(ty) + take(m) + take(s) + take(s)
    order += take(q, 2) + take(v) + take(m) + take(o) + take(q, 2) + take(v)
    return order


RING_KINDS = "OQVRTY"


def ring_counts(kind, i, r):
    return {
        "O": (16, 4 * (r - 1) + i + 1),
        "Q": (8, 4 * (r // 2 + 1) + i + 1),
        "V": (4, 2 * (r // 2 + 1) + i + 1),
        "R": (4, r + 2),
        "T": (4, 2 * (r // 2 - 1) + i + 1),
        "Y": (4, 2 * (r // 2 - 1) + i + 1),
    }[kind]


def ring_uses(first, last):
    return [((r, k, i), (k, *ring_counts(k, i, r))) for r in range(4) for k, i in step_order(r, first, last)
            if k in RING_KINDS]


def ring_plan():
    pro = [((0, "Q", i), ("Q", 0, i + 1)) for i in range(4)] + [((0, "V", i), ("V", 0, i + 1)) for i in range(2)]
    pro += [((0, "R", 0), ("R", 0, 1))]
    first, mid, last = ring_uses(True, False), ring_uses(False, False), ring_uses(False, True)
    epi = [((4, "O", k), ("O", 16, 12 + k + 1)) for k in range(4)]
    epi += [((5, k, c), (k, 4, 2 + c + 1)) for c in range(2) for k in "TY"]
    back = [(key, (k, a, c - a)) for key, (k, a, c) in mid]
    assert len(mid) % 2 == 0 and len(first) % 2 == 0
    plans = {}
    for name, before, uses, at in (("pro", [], pro, 1), ("first", pro, first, 0), ("mid", back, mid, 0),
                                   ("last", back, last, 0), ("epi", last, epi, len(last))):
        both = before + uses
        n0 = len(before)
        plans[name] = {
            key: ((at + n) % 2, both[n0 + n - 2][1] if n0 + n >= 2 else None) for n, (key, _) in enumerate(uses)
        }
    return plans


def build(nc, x_d, wqkv_d, wout_d, rw_d, rb_d, w1_d, b1_d, w2_d, b2_d, out_d):
    B, L, D = x_d.shape
    HD = wout_d.shape[0]
    DH = 64
    NPAIR = HD // P
    NE, _, F = w1_d.shape
    NT = B * L // P
    IT = L // P
    FT = F // P
    OFF = [sum(L - P * a for a in range(j)) for j in range(IT)]
    PW = OFF[-1] + P
    VC = 3 * DH + 1
    SCALE = DH ** -0.5
    assert B == 2 and IT == 8 and D == P and FT == 4 and NE == 8
    RING = ring_plan()

    with ExitStack() as ctx:
        def sb(name, shape, dt=F32):
            return ctx.enter_context(nc.sbuf_tensor(name, shape, dt))

        def sem(name):
            return ctx.enter_context(nc.semaphore(name))

        ps_s = ctx.enter_context(nc.psum_tensor("ps_s", [P, 2, 2 * 512], F32))
        ps_m = ctx.enter_context(nc.psum_tensor("ps_m", [P, 2 * 512], F32))
        ps_r = ctx.enter_context(nc.psum_tensor("ps_r", [P, 2, 512], F32))

        x_sb = sb("x_sb", [P, NT, D])
        xn = sb("xn", [P, NT, D])
        xnT = sb("xnT", [P, NT * P])
        y_acc = sb("y_acc", [P, NT, D])
        identf = sb("identf", [P, P])
        identb = sb("identb", [P, P], BF16)
        mask_rows = sb("mask_rows", [P, L])
        mask_cols = sb("mask_cols", [P, P], BF16)
        stats = sb("stats", [P, NT, 6])
        meanvar = sb("meanvar", [P, NT, 2])
        vareps = sb("vareps", [P, NT])
        std = sb("std", [P, NT])
        rstd = sb("rstd", [P, NT])

        s_x = sem("s_x")
        s_const = sem("s_const")
        s_pool = sem("s_pool")
        s_dve = sem("s_dve")
        s_var = sem("s_var")
        s_std = sem("s_std")
        s_xn = sem("s_xn")
        s_xt_full = sem("s_xt_full")
        s_xt = sem("s_xt")

        w_loaded = [sem(f"w_loaded{b}") for b in range(2)]
        s_wout = sem("s_wout")
        full = {k: sem(f"full_{k}") for k in "SMOQVRTY"}
        freed = {k: sem(f"freed_{k}") for k in "OQVRTY"}
        s_hi = sem("s_hi")
        s_q_stacked = sem("s_q_stacked")
        s_k_stacked = sem("s_k_stacked")
        s_v1 = sem("s_v1")
        s_v2 = sem("s_v2")
        s_v3 = sem("s_v3")
        s_max = sem("s_max")
        s_carry = sem("s_carry")
        s_mh = sem("s_mh")
        s_m_rows = sem("s_m_rows")
        s_exp = sem("s_exp")
        s_plo = sem("s_plo")
        s_rec = sem("s_rec")
        s_o = sem("s_o")

        main = ExitStack()
        with main:
            def sbm(name, shape, dt=F32):
                return main.enter_context(nc.sbuf_tensor(name, shape, dt))

            W = sbm("W", [P, 2, 3, P])
            wout = sbm("wout", [P, NPAIR * D])
            T1 = sbm("T1", [P, 2, 2, L], F32R)
            T2 = sbm("T2", [P, 2, 2, L], F32R)
            K1 = sbm("K1", [P, 2, 2, L], F32R)
            K2 = sbm("K2", [P, 2, 2, L], F32R)
            q_lo = sbm("q_lo", [P, L], F32R)
            vparts = sbm("vparts", [P, 2, IT, 2, VC + 1], BF16)
            v_rest = sbm("v_rest", [P, 2, 4, P])
            probs = sbm("probs", [P, 2, PW])
            probs_lo = sbm("probs_lo", [P, 2, PW], F16)
            junk = sbm("junk", [P, 2, L], BF16)
            mx = sbm("mx", [P, 2, IT])
            mh = sbm("mh", [IT, 2, P], F32R)
            ml = sbm("ml", [IT, 2, P], F32R)
            rec = sbm("rec", [P, IT])
            o_raw = sbm("o_raw", [P, 2, 2, DH])
            o_sb = sbm("o_sb", [P, 2, IT, P])
            oT = sbm("oT", [P, 2, 512])

            probs_hi = probs[:].bitcast(BF16).rearrange("p g (n t) -> p g n t", t=2)[:, :, :, 1]
            OWN = [(0, 64), (64, 128)]
            OTHER = [(64, 128), (0, 64)]

            def w_slice(p):
                return wqkv_d.rearrange("r (t p c) -> r t p c", t=3, p=NPAIR)[:, :, bass.ds(p, 1), :].rearrange(
                    "r t p c -> r t (p c)")

            block = main.enter_context(nc.Block())

            def run_bodies(eng, body):
                body(0, "first")
                with eng.Fori(1, NPAIR - 1) as p:
                    body(p, "mid")
                body(NPAIR - 1, "last")

            def stages(name):
                for r in range(4):
                    for kind, i in step_order(r, name == "first", name == "last"):
                        yield r, kind, i

            @block.sync
            def _(sp):
                sp.dma_start(x_sb[:], x_d.rearrange("b (t p) d -> p (b t) d", p=P)).then_inc(s_x, 16)
                for b in range(2):
                    sp.dma_start(W[:, b], w_slice(0)).then_inc(w_loaded[b], 16)
                sp.dma_start(wout[:].rearrange("r (p n) -> r p n", n=D),
                             wout_d.rearrange("(p r) n -> r p n", r=P)).then_inc(s_wout, 16)

                def stack_q(u, b):
                    sp.wait_ge(freed["Q"], 4 * u + 2)
                    for s in range(2):
                        (o0, o1), (t0, t1) = OWN[s], OTHER[s]
                        sp.dma_start(T1[t0:t1, b, s, :].bitcast(F32), q_lo[o0:o1, :].bitcast(F32)).then_inc(s_q_stacked, 16)
                        sp.dma_start(T2[o0:o1, b, s, :].bitcast(F32), T1[o0:o1, b, s, :].bitcast(F32)).then_inc(s_q_stacked, 16)

                def stack_k(u, b):
                    sp.wait_ge(freed["Q"], 4 * u + 4)
                    for s in range(2):
                        (o0, o1), (t0, t1) = OWN[s], OTHER[s]
                        sp.dma_start(K1[t0:t1, b, s, :].bitcast(F32), K1[o0:o1, b, s, :].bitcast(F32)).then_inc(s_k_stacked, 16)

                def max_rows(g, b, s):
                    sp.wait_ge(freed["R"], g + 1)
                    t0 = OTHER[s][0]
                    for n, part in enumerate((mh, ml)):
                        sp.dma_start(T2[t0 + n:t0 + n + 1, b, s, :].bitcast(F32).rearrange(
                            "o (t i) -> o t i", i=P), part[:, s, :].bitcast(F32)).then_inc(s_m_rows, 16)

                stack_q(0, 0)
                stack_k(0, 0)
                max_rows(0, 0, 0)

                def body(p, name):
                    for r, kind, i in stages(name):
                        u1 = 2 * p + r // 2 + 1
                        b1 = (r // 2 + 1) % 2
                        if r in (0, 2) and (kind, i) == ("S", 0) and name != "last":
                            b = r // 2
                            sp.wait_ge(full["V"], 4 * p + 2 * b + 2)
                            sp.dma_start(W[:, b], w_slice(p + 1)).then_inc(w_loaded[b], 16)
                        if (kind, i) == ("Q", 1):
                            stack_q(u1, b1)
                        if (kind, i) == ("Q", 3):
                            stack_k(u1, b1)
                        if kind == "R":
                            max_rows(4 * p + r + 1, (r + 1) // 2 % 2, (r + 1) % 2)

                run_bodies(sp, body)

            @block.gpsimd
            def _(pool):
                n = [0]

                def link(ins):
                    n[0] += 1
                    ins.then_inc(s_pool, 1)
                    pool.wait_ge(s_pool, n[0])

                link(pool.memset(identf[:], 0.0))
                link(pool.affine_select(out=identf[:], in_=identf[:], compare_op=ALU.not_equal, fill=1.0, base=0,
                                        pattern=[[-1, P]], channel_multiplier=1))
                pool.tensor_copy(identb[:], identf[:]).then_inc(s_const, 1)
                pool.memset(T2[:].bitcast(F32), 0.0).then_inc(s_const, 1)
                pool.memset(y_acc[:], 0.0).then_inc(s_const, 1)
                link(pool.memset(K2[:].bitcast(F32), 0.0))
                for s in range(2):
                    t0 = OTHER[s][0]
                    pool.memset(K2[t0:t0 + 2, :, s, :].bitcast(F32), 1.0).then_inc(s_const, 1)
                    pool.wait_ge(s_const, 4 + s)
                link(pool.memset(mask_rows[:], 0.0))
                pool.affine_select(out=mask_rows[:, L - P:], in_=mask_rows[:, L - P:], compare_op=ALU.is_ge, fill=NEG,
                                   base=0, pattern=[[-1, P]], channel_multiplier=1).then_inc(s_const, 1)
                link(pool.memset(mask_cols[:], 0.0))
                pool.affine_select(out=mask_cols[:], in_=mask_cols[:], compare_op=ALU.is_ge, fill=NEG,
                                   base=0, pattern=[[1, P]], channel_multiplier=-1).then_inc(s_const, 1)
                pool.memset(vparts[:, :, :, :, VC - 1:VC + 1], 1.0).then_inc(s_const, 1)

                def v_low(u, b, i):
                    pool.wait_ge(s_v2, 2 * u + i + 1)
                    pool.tensor_tensor(vparts[:, b, 4 * i:4 * i + 4, :, 0:DH],
                                       v_rest[:, i].rearrange("p t (s d) -> p t s d", s=2),
                                       vparts[:, b, 4 * i:4 * i + 4, :, DH:2 * DH],
                                       ALU.subtract).then_inc(s_v3, 1)

                def p_low(g, s, j):
                    w = L - P * j
                    pool.wait_ge(s_exp, 8 * g + j + 1)
                    pool.tensor_tensor(probs_lo[:, s, OFF[j]:OFF[j] + w], probs[:, s, OFF[j]:OFF[j] + w],
                                       probs_hi[:, s, OFF[j]:OFF[j] + w], ALU.subtract).then_inc(s_plo, 1)

                for i in range(2):
                    v_low(0, 0, i)

                def body(p, name):
                    for r, kind, i in stages(name):
                        if kind == "S":
                            p_low(4 * p + r, r % 2, i)
                        if kind == "V":
                            v_low(2 * p + r // 2 + 1, (r // 2 + 1) % 2, i)

                run_bodies(pool, body)

            @block.vector
            def _(dve):
                n = [0]

                def link(ins):
                    n[0] += 1
                    ins.then_inc(s_dve, 1)
                    dve.wait_ge(s_dve, n[0])

                dve.wait_ge(s_x, 16)
                for t in range(NT):
                    last = dve.bn_stats(stats[:, t, :], x_sb[:, t, :])
                link(last)
                for t in range(NT):
                    last = dve.bn_aggr(meanvar[:, t, :], stats[:, t, :])
                link(last)
                dve.tensor_scalar(vareps[:], meanvar[:, :, 1], EPS, None, ALU.add).then_inc(s_var, 1)
                dve.wait_ge(s_std, 1)
                link(dve.reciprocal(rstd[:], std[:]))
                for t in range(NT):
                    dve.tensor_scalar(xn[:, t, :], x_sb[:, t, :], meanvar[:, t, 0:1], rstd[:, t:t + 1],
                                      ALU.subtract, ALU.mult).then_inc(s_xn, 1)
                for c in range(0, 4):
                    dve.wait_ge(s_xt_full, 4 * c + 4)
                    dve.tensor_copy(xnT[:, 512 * c:512 * c + 512], ps_s[:, c // 2, 512 * (c % 2):512 * (c % 2) + 512]
                                    ).then_inc(s_xt, 1)

                dve.wait_ge(s_const, 8)

                def q_low(u, b, i, bank):
                    dve.wait_ge(s_hi, 4 * u + i + 1)
                    c = 512 * (i % 2)
                    for s in range(2):
                        o0, o1 = OWN[s]
                        hi = (T1 if i < 2 else K1)[o0:o1, b, s, c:c + 512].bitcast(F32)
                        dst = q_lo[o0:o1, c:c + 512] if i < 2 else K2[o0:o1, b, s, c:c + 512]
                        last = dve.tensor_tensor(dst, ps_r[o0:o1, bank, :], hi, ALU.subtract)
                    last.then_inc(freed["Q"], 1)

                def v_split(u, b, i, bank):
                    dve.wait_ge(s_v1, 2 * u + i + 1)
                    dve.tensor_tensor(v_rest[:, i].rearrange("p t (s d) -> p t s d", s=2),
                                      ps_r[:, bank, :].rearrange("p (t s d) -> p t s d", t=4, s=2),
                                      vparts[:, b, 4 * i:4 * i + 4, :, 2 * DH:3 * DH],
                                      ALU.subtract).then_inc(freed["V"], 1)
                    dve.wait_ge(freed["V"], 2 * u + i + 1)
                    dve.tensor_copy(vparts[:, b, 4 * i:4 * i + 4, :, DH:2 * DH],
                                    v_rest[:, i].rearrange("p t (s d) -> p t s d", s=2)).then_inc(s_v2, 1)

                def row_max(g, s, i):
                    w = P * (i + 1)
                    dve.wait_ge(full["M"], 8 * g + i + 1)
                    dve.sem_inc(s_carry, 1)
                    at = 512 * (i % 2) if i < 4 else 0
                    dve.tensor_tensor_reduce(junk[:, i % 2, 0:w], ps_m[:, at:at + w], mask_rows[:, L - w:L], 1.0, -3.0e38,
                                             ALU.add, ALU.max, mx[:, s, i:i + 1]).then_inc(s_max, 1)

                def max_split(g, s, bank):
                    dve.wait_ge(full["R"], g + 1)
                    dve.tensor_scalar(mh[:, s, :], ps_r[0:IT, bank, 0:P], -1.0, None, ALU.mult).then_inc(s_mh, 1)
                    dve.wait_ge(s_mh, g + 1)
                    dve.scalar_tensor_tensor(ml[:, s, :], ps_r[0:IT, bank, 0:P], -1.0, mh[:, s, :].bitcast(F32),
                                             ALU.mult, ALU.subtract).then_inc(freed["R"], 1)

                def normalise(g, b, s, k, bank):
                    dve.wait_ge(full["O"], 4 * g + k + 1)
                    both = ps_r[:, bank, 0:2 * VC].rearrange("p (t c) -> p t c", t=2)
                    dve.reciprocal(rec[:, 2 * k:2 * k + 2], both[:, :, VC - 1]).then_inc(s_rec, 1)
                    dve.tensor_reduce(o_raw[:, k % 2], both[:, :, 0:3 * DH].rearrange("p t (a d) -> p t d a", a=3), AX_X,
                                      ALU.add).then_inc(freed["O"], 1)
                    dve.wait_ge(s_rec, 4 * g + k + 1)
                    dve.wait_ge(freed["O"], 4 * g + k + 1)
                    dve.tensor_tensor(o_sb[:, b, 2 * k:2 * k + 2, DH * s:DH * s + DH], o_raw[:, k % 2],
                                      rec[:, 2 * k:2 * k + 2].unsqueeze(2).to_broadcast([P, 2, DH]),
                                      ALU.mult).then_inc(s_o, 1)

                def accumulate(u, b, c, bank):
                    dve.wait_ge(full["Y"], 2 * u + c + 1)
                    ya = y_acc[:, IT * b + 4 * c:IT * b + 4 * c + 4, :]
                    dve.tensor_tensor(ya, ps_r[:, bank, :].rearrange("p (t d) -> p t d", t=4), ya,
                                      ALU.add).then_inc(freed["Y"], 1)

                for i in range(4):
                    if i == 2:
                        pass
                    q_low(0, 0, i, RING["pro"][(0, "Q", i)][0])
                for i in range(2):
                    v_split(0, 0, i, RING["pro"][(0, "V", i)][0])
                for i in range(8):
                    row_max(0, 0, i)
                max_split(0, 0, RING["pro"][(0, "R", 0)][0])

                def body(p, name):
                    for r, kind, i in stages(name):
                        g = 4 * p + r
                        u1, b1 = 2 * p + r // 2 + 1, (r // 2 + 1) % 2
                        bank = RING[name][(r, kind, i)][0] if kind in RING_KINDS else None
                        if kind == "M":
                            if i == 0 and not (name == "first" and r == 0):
                                dve.wait_ge(full["R"], g)
                            row_max(g + 1, (r + 1) % 2, i)
                        if kind == "R":
                            if not (name == "first" and r == 0):
                                dve.wait_ge(s_m_rows, 32 * g)
                            max_split(g + 1, (r + 1) % 2, bank)
                        if kind == "O":
                            normalise(g - 1, (r - 1) // 2 % 2, (r - 1) % 2, i, bank)
                        if kind == "Q":
                            if i == 0:
                                dve.wait_ge(s_q_stacked, 64 * u1)
                            q_low(u1, b1, i, bank)
                        if kind == "V":
                            dve.wait_ge(s_v3, 2 * u1 + i - 1)
                            v_split(u1, b1, i, bank)
                        if kind == "Y":
                            accumulate(u1 - 2, b1, i, bank)

                run_bodies(dve, body)
                for k in range(4):
                    normalise(4 * NPAIR - 1, 1, 1, k, RING["epi"][(4, "O", k)][0])
                for c in range(2):
                    dve.wait_ge(freed["Y"], 2 * (2 * NPAIR - 3) + c + 1)
                    accumulate(2 * NPAIR - 1, 1, c, RING["epi"][(5, "Y", c)][0])

            @block.scalar
            def _(act):
                act.wait_ge(s_var, 1)
                act.activation(std[:], vareps[:], ACT.Sqrt).then_inc(s_std, 1)

                def q_high(u, b, i, bank):
                    act.wait_ge(full["Q"], 4 * u + i + 1)
                    c = 512 * (i % 2)
                    for s in range(2):
                        o0, o1 = OWN[s]
                        last = act.activation((T1 if i < 2 else K1)[o0:o1, b, s, c:c + 512], ps_r[o0:o1, bank, :],
                                              ACT.Copy)
                    last.then_inc(s_hi, 1)

                def v_high(u, b, i, bank):
                    act.wait_ge(full["V"], 2 * u + i + 1)
                    act.activation(vparts[:, b, 4 * i:4 * i + 4, :, 2 * DH:3 * DH],
                                   ps_r[:, bank, :].rearrange("p (t s d) -> p t s d", t=4, s=2),
                                   ACT.Copy).then_inc(s_v1, 1)

                def exps(g, s, j):
                    w = L - P * j
                    act.wait_ge(full["S"], 8 * g + j + 1)
                    act.activation(probs[:, s, OFF[j]:OFF[j] + w], ps_s[:, j % 2, 0:w], ACT.Exp,
                                   scale=SCALE).then_inc(s_exp, 1)

                def o_turned(u, c, bank):
                    act.wait_ge(full["T"], 2 * u + c + 1)
                    act.activation(oT[:, c, :], ps_r[:, bank, :], ACT.Copy).then_inc(freed["T"], 1)

                for i in range(4):
                    q_high(0, 0, i, RING["pro"][(0, "Q", i)][0])
                for i in range(2):
                    v_high(0, 0, i, RING["pro"][(0, "V", i)][0])

                def body(p, name):
                    for r, kind, i in stages(name):
                        g = 4 * p + r
                        u1, b1 = 2 * p + r // 2 + 1, (r // 2 + 1) % 2
                        bank = RING[name][(r, kind, i)][0] if kind in RING_KINDS else None
                        if kind == "S":
                            if i == 0 and not (name == "first" and r < 2):
                                act.wait_ge(full["O"], 4 * g - 4)
                            exps(g, r % 2, i)
                        if kind == "Q":
                            q_high(u1, b1, i, bank)
                        if kind == "V":
                            v_high(u1, b1, i, bank)
                        if kind == "T":
                            o_turned(u1 - 2, i, bank)

                run_bodies(act, body)
                for c in range(2):
                    o_turned(2 * NPAIR - 1, c, RING["epi"][(5, "T", c)][0])

            @block.tensor
            def _(pe):
                def wait_bank(use, p):
                    if use is not None:
                        kind, a, c = use
                        pe.wait_ge(freed[kind], a * p + c)

                def project(u, b, i, bank):
                    if i == 0:
                        pe.wait_ge(w_loaded[b], 16 * (u // 2 + 1) if isinstance(u, int) else 8 * u + (16 if b == 0 else 8))
                    t = i // 2
                    tok = L * b + 512 * (i % 2)
                    pe.matmul(ps_r[:, bank, :], W[:, b, t, :], xnT[:, tok:tok + 512], start=True, stop=True
                              ).then_inc(full["Q"], 1)

                def values(u, b, i, bank):
                    for t in range(4):
                        tok = L * b + P * (4 * i + t)
                        last = pe.matmul(ps_r[:, bank, P * t:P * t + P], xnT[:, tok:tok + P], W[:, b, 2, :],
                                         start=True, stop=True)
                    last.then_inc(full["V"], 1)

                def max_scores(g, u, b, s, i):
                    if i == 0:
                        pe.wait_ge(s_q_stacked, 64 * u + 64)
                        pe.wait_ge(s_k_stacked, 32 * u + 32)
                    w = P * (i + 1)
                    at = 512 * (i % 2) if i < 4 else 0
                    for c in range(0, w, 512):
                        m = min(512, w - c)
                        last = pe.matmul(ps_m[:, at + c:at + c + m], T1[:, b, s, P * i:P * i + P],
                                         K1[:, b, s, c:c + m], start=True, stop=True)
                    last.then_inc(full["M"], 1)

                MAX_BEFORE = [0, 0, 1, 2, 4, 5, 6, 7]

                def max_turned(g, s, bank):
                    pe.wait_ge(s_max, 8 * g + 8)
                    pe.transpose(ps_r[0:IT, bank, 0:P], mx[:, s, :], identf[:]).then_inc(full["R"], 1)

                def scores(g, b, s, j):
                    if j == 0:
                        pe.wait_ge(s_m_rows, 32 * g + 32)
                    w = L - P * j
                    for c in range(0, w, 512):
                        m = min(512, w - c)
                        i0 = P * j + c
                        dst = ps_s[:, j % 2, c:c + m]
                        pe.matmul(dst, K1[:, b, s, P * j:P * j + P], T1[:, b, s, i0:i0 + m], start=True, stop=False,
                                  skip_group_check=True)
                        last = pe.matmul(dst, K2[:, b, s, P * j:P * j + P], T2[:, b, s, i0:i0 + m], start=False,
                                         stop=c > 0, skip_group_check=True)
                        if c == 0:
                            last = pe.matmul(ps_s[:, j % 2, 0:P], identb[:], mask_cols[:], start=False, stop=True,
                                             skip_group_check=True)
                    last.then_inc(full["S"], 1)

                def value_products(g, b, s, k, bank):
                    pe.wait_ge(s_plo, 8 * g + 2 * k + 2)
                    for e in range(2):
                        it = 2 * k + e
                        for j in range(it + 1):
                            at = OFF[j] + P * (it - j)
                            pe.matmul(ps_r[:, bank, VC * e:VC * e + VC], probs_hi[:, s, at:at + P],
                                      vparts[:, b, j, s, 0:VC], start=j == 0, stop=False, skip_group_check=True)
                            last = pe.matmul(ps_r[:, bank, VC * e + DH:VC * e + VC], probs_lo[:, s, at:at + P],
                                             vparts[:, b, j, s, DH:VC], start=False, stop=j == it,
                                             skip_group_check=True)
                    last.then_inc(full["O"], 1)

                def turn_outputs(u, b, c, bank):
                    pe.wait_ge(s_o, 8 * u + 4 + 2 * c + 2)
                    for t in range(4):
                        last = pe.transpose(ps_r[:, bank, P * t:P * t + P], o_sb[:, b, 4 * c + t, :], identf[:])
                    last.then_inc(full["T"], 1)

                def out_project(u, b, c, p, bank):
                    pe.wait_ge(freed["T"], 2 * u + c + 1)
                    for t in range(4):
                        last = pe.matmul(ps_r[:, bank, P * t:P * t + P], oT[:, c, P * t:P * t + P],
                                         wout[:, bass.ts(p, D)], start=True, stop=True)
                    last.then_inc(full["Y"], 1)

                pe.wait_ge(s_const, 8)
                for t in range(NT):
                    pe.wait_ge(s_xn, t + 1)
                    pe.transpose(ps_s[:, t // 8, P * (t % 8):P * (t % 8) + P], xn[:, t, :], identf[:]
                                 ).then_inc(s_xt_full, 1)
                pe.wait_ge(s_xt, 4)
                for i in range(4):
                    bank, use = RING["pro"][(0, "Q", i)]
                    wait_bank(use, 0)
                    project(0, 0, i, bank)
                for i in range(2):
                    bank, use = RING["pro"][(0, "V", i)]
                    wait_bank(use, 0)
                    values(0, 0, i, bank)
                for i in range(8):
                    if MAX_BEFORE[i]:
                        pe.wait_ge(s_max, MAX_BEFORE[i])
                    max_scores(0, 0, 0, 0, i)
                bank, use = RING["pro"][(0, "R", 0)]
                wait_bank(use, 0)
                max_turned(0, 0, bank)
                pe.wait_ge(s_wout, 16)

                def body(p, name):
                    for r, kind, i in stages(name):
                        g = 4 * p + r
                        u1, b1 = 2 * p + r // 2 + 1, (r // 2 + 1) % 2
                        if kind in RING_KINDS:
                            bank, use = RING[name][(r, kind, i)]
                            wait_bank(use, p)
                        if kind == "S":
                            if not (name == "first" and r == 0 and i < 2):
                                pe.wait_ge(s_exp, 8 * g + i - 1)
                            scores(g, (r // 2) % 2, r % 2, i)
                        if kind == "M":
                            pe.wait_ge(s_max, 8 * (g + 1) + MAX_BEFORE[i])
                            max_scores(g + 1, 2 * p + (r + 1) // 2, (r + 1) // 2 % 2, (r + 1) % 2, i)
                        if kind == "R":
                            max_turned(g + 1, (r + 1) % 2, bank)
                        if kind == "O":
                            if i == 0 and (r - 1) % 2 == 0:
                                pe.wait_ge(s_v3, 2 * (2 * p + (r - 1) // 2) + 2)
                            value_products(g - 1, (r - 1) // 2 % 2, (r - 1) % 2, i, bank)
                        if kind == "Q":
                            project(u1, b1, i, bank)
                        if kind == "V":
                            values(u1, b1, i, bank)
                        if kind == "T":
                            turn_outputs(u1 - 2, b1, i, bank)
                        if kind == "Y":
                            out_project(u1 - 2, b1, i, p - 1 if r == 1 else p, bank)

                run_bodies(pe, body)
                for k in range(4):
                    bank, use = RING["epi"][(4, "O", k)]
                    wait_bank(use, NPAIR - 1)
                    value_products(4 * NPAIR - 1, 1, 1, k, bank)
                for c in range(2):
                    bank, use = RING["epi"][(5, "T", c)]
                    wait_bank(use, NPAIR - 1)
                    turn_outputs(2 * NPAIR - 1, 1, c, bank)
                    bank, use = RING["epi"][(5, "Y", c)]
                    wait_bank(use, NPAIR - 1)
                    out_project(2 * NPAIR - 1, 1, c, NPAIR - 1, bank)

        moe(nc, ctx, sb, sem, x_sb, xn, xnT, y_acc, identf, stats, meanvar, vareps, std, rstd, ps_s, ps_m, ps_r,
            rw_d, rb_d, w1_d, b1_d, w2_d, b2_d, out_d, NT, D, NE, F, FT)


def moe(nc, ctx, sb, sem, x_sb, xn, xnT, acc, identf, stats, meanvar, vareps, std, rstd, ps_s, ps_m, ps_r,
        rw_d, rb_d, w1_d, b1_d, w2_d, b2_d, out_d, NT, D, NE, F, FT):
    rw = sb("rw", [P, NE])
    rb = sb("rb", [P, NE])
    b1r = sb("b1r", [NE * FT, P])
    b1T = sb("b1T", [P, NE * FT])
    b2 = sb("b2", [NE, D])
    logits = sb("logits", [P, NT, NE])
    w8 = sb("w8", [P, NT, NE])
    down = sb("down", [P, NE])
    mxl = sb("mxl", [P, NT])
    den = sb("den", [P, NT])
    ptop = sb("ptop", [P, NT])
    gates = sb("gates", [P, NT, NE])
    gT = sb("gT", [NE, NT * P])
    w1 = sb("w1", [P, 2, F])
    w2 = sb("w2", [P, 2, FT, D])
    hT = sb("hT", [P, 2, FT, 512])

    s_small = sem("s_small")
    s_w12 = [sem(f"s_w12_{w}") for w in range(2)]
    s_d = sem("s_d")
    s_down = sem("s_down")
    s_var2 = sem("s_var2")
    s_std2 = sem("s_std2")
    s_x2n = sem("s_x2n")
    s_tr = sem("s_tr")
    s_x2T = sem("s_x2T")
    s_log = sem("s_log")
    s_dif = sem("s_dif")
    s_ex = sem("s_ex")
    s_gate = sem("s_gate")
    s_gTf = sem("s_gTf")
    s_gT = sem("s_gT")
    s_b1f = sem("s_b1f")
    s_init = sem("s_init")
    s_h = sem("s_h")
    relu_act = sem("relu_act")
    relu_dve = sem("relu_dve")
    s_y2 = sem("s_y2")
    s_carry2 = sem("s_carry2")
    s_acc = sem("s_acc")
    s_res = sem("s_res")
    s_out = sem("s_out")

    NC = NT // 4
    with nc.Block() as block:
        @block.sync
        def _(sp):
            with nc.allow_non_contiguous_dma(reason="small"):
                sp.dma_start(rb[:], rb_d.partition_broadcast(P)).then_inc(s_small, 16)
            sp.dma_start(rw[:], rw_d).then_inc(s_small, 16)
            sp.dma_start(b1r[:], b1_d.rearrange("e (f q) -> (e f) q", q=P)).then_inc(s_small, 16)
            sp.dma_start(b2[:], b2_d).then_inc(s_small, 16)

            def load(e, w):
                sp.dma_start(w1[:, w, :], w1_d[bass.ds(e, 1)].rearrange("e r f -> r (e f)")).then_inc(s_w12[w], 16)
                sp.dma_start(w2[:, w], w2_d[bass.ds(e, 1)].rearrange("e (f q) d -> q (e f) d", q=P)
                             ).then_inc(s_w12[w], 16)

            load(0, 0)
            load(1, 1)
            with sp.Fori(0, NE // 2 - 1) as q:
                for w in range(2):
                    sp.wait_ge(s_y2, 8 * q + 4 * w + 4 + 2)
                    load(2 * q + w + 2, w)
            for c in range(NC):
                sp.wait_ge(s_res, c + 1)
                sp.dma_start(out_d.rearrange("b (t p) d -> p (b t) d", p=P)[:, 4 * c:4 * c + 4, :],
                             x_sb[:, 4 * c:4 * c + 4, :]).then_inc(s_out, 16)
            sp.wait_ge(s_out, 16 * NC)

        @block.gpsimd
        def _(pool):
            pool.iota(down[:], [[-1, NE]], base=NE, channel_multiplier=0,
                      allow_small_or_imprecise_dtypes=True).then_inc(s_down, 1)

        @block.vector
        def _(dve):
            n = [0]

            def link(ins):
                n[0] += 1
                ins.then_inc(s_d, 1)
                dve.wait_ge(s_d, n[0])

            def normalise(src, dst, k):
                for t in range(NT):
                    last = dve.bn_stats(stats[:, t, :], src[:, t, :])
                link(last)
                for t in range(NT):
                    last = dve.bn_aggr(meanvar[:, t, :], stats[:, t, :])
                link(last)
                dve.tensor_scalar(vareps[:], meanvar[:, :, 1], EPS, None, ALU.add).then_inc(s_var2, 1)
                dve.wait_ge(s_std2, k)
                link(dve.reciprocal(rstd[:], std[:]))
                for t in range(NT):
                    last = dve.tensor_scalar(dst[:, t, :], src[:, t, :], meanvar[:, t, 0:1], rstd[:, t:t + 1],
                                             ALU.subtract, ALU.mult)
                return last

            link(normalise(acc, xn, 1))
            link(dve.tensor_tensor(x_sb[:], x_sb[:], xn[:], ALU.add))
            normalise(x_sb, xn, 2).then_inc(s_x2n, 1)
            for c in range(NC):
                dve.wait_ge(s_tr, c + 1)
                dve.tensor_copy(xnT[:, 512 * c:512 * c + 512], ps_s[:, c // 2, 512 * (c % 2):512 * (c % 2) + 512]
                                ).then_inc(s_x2T, 1)
            dve.wait_ge(s_b1f, 1)
            dve.tensor_copy(b1T[:], ps_m[:, 0:NE * FT])
            dve.wait_ge(s_log, 1)
            dve.wait_ge(s_small, 64)
            link(dve.tensor_tensor(logits[:], ps_r[:, 0, 0:NT * NE].rearrange("p (t e) -> p t e", e=NE),
                                   rb[:].unsqueeze(1).to_broadcast([P, NT, NE]), ALU.add))
            link(dve.tensor_reduce(mxl[:], logits[:], AX_X, ALU.max))
            dve.tensor_tensor(logits[:], logits[:], mxl[:].unsqueeze(2).to_broadcast([P, NT, NE]), ALU.subtract
                              ).then_inc(s_dif, 1)
            dve.wait_ge(s_dif, 1)
            dve.wait_ge(s_down, 1)
            link(dve.tensor_scalar(w8[:], logits[:], 0.0, None, ALU.is_ge))
            link(dve.tensor_tensor(w8[:], w8[:], down[:].unsqueeze(1).to_broadcast([P, NT, NE]), ALU.mult))
            link(dve.tensor_reduce(mxl[:], w8[:], AX_X, ALU.max))
            link(dve.tensor_tensor(w8[:], w8[:], mxl[:].unsqueeze(2).to_broadcast([P, NT, NE]), ALU.is_equal))
            dve.wait_ge(s_ex, 1)
            link(dve.tensor_reduce(den[:], gates[:], AX_X, ALU.add))
            link(dve.reciprocal(ptop[:], den[:]))
            dve.tensor_tensor(gates[:], w8[:], ptop[:].unsqueeze(2).to_broadcast([P, NT, NE]), ALU.mult
                              ).then_inc(s_gate, 1)
            for c in range(NC):
                dve.wait_ge(s_gTf, c + 1)
                dve.tensor_copy(gT[:, 512 * c:512 * c + 512],
                                ps_s[0:NE, c // 2, 512 * (c % 2):512 * (c % 2) + 512]).then_inc(s_gT, 1)
            for c in range(NC):
                dve.wait_ge(s_init, c + 1)
                last = dve.tensor_copy(acc[:, 4 * c:4 * c + 4, :], ps_r[:, c % 2, :].rearrange("p (t d) -> p t d", t=4))
                last.then_inc(s_acc, 1)
            dve.wait_ge(s_acc, NC)
            dve.tensor_copy(b1T[:], b1T[:]).then_inc(relu_dve, 2)
            dve.wait_ge(relu_dve, 2)
            with dve.Fori(0, NE // 2) as q:
                for w in range(2):
                    for c in range(NC):
                        chunk = 8 * q + 4 * w + c
                        dve.wait_ge(s_y2, chunk + 1)
                        for f in (1, 3):
                            dve.wait_ge(s_h, 4 * chunk + f + 1)
                            dve.tensor_scalar(hT[:, c % 2, f, :], ps_s[:, f // 2, 512 * (f % 2):512 * (f % 2) + 512],
                                              b1T[:, bass.ds(8 * q + 4 * w + f, 1)], 0.0, ALU.add, ALU.max
                                              ).then_inc(relu_dve, 1)
                        dve.wait_ge(s_y2, chunk + 3)
                        dve.wait_ge(s_acc, chunk + 1)
                        for t in range(4):
                            last = dve.scalar_tensor_tensor(
                                acc[:, 4 * c + t, :], ps_m[:, 512 * (c % 2) + P * t:512 * (c % 2) + P * t + P],
                                gates[:, 4 * c + t, bass.ds(2 * q + w, 1)], acc[:, 4 * c + t, :], ALU.mult, ALU.add)
                        last.then_inc(s_acc, 1)
            dve.wait_ge(s_acc, NC + NC * NE)
            link(normalise(acc, xn, 3))
            for c in range(NC):
                dve.tensor_tensor(x_sb[:, 4 * c:4 * c + 4, :], x_sb[:, 4 * c:4 * c + 4, :], xn[:, 4 * c:4 * c + 4, :],
                                  ALU.add).then_inc(s_res, 1)

        @block.scalar
        def _(act):
            for k in range(2):
                act.wait_ge(s_var2, k + 1)
                act.activation(std[:], vareps[:], ACT.Sqrt).then_inc(s_std2, 1)
            act.wait_ge(s_dif, 1)
            act.activation(gates[:], logits[:], ACT.Exp).then_inc(s_ex, 1)
            act.wait_ge(relu_dve, 2)
            act.activation(den[:, 0:1], den[:, 0:1], ACT.Copy).then_inc(relu_act, 2)
            with act.Fori(0, NE // 2) as q:
                for w in range(2):
                    for c in range(NC):
                        chunk = 8 * q + 4 * w + c
                        for f in (0, 2):
                            act.wait_ge(s_y2, chunk + 1)
                            act.wait_ge(s_h, 4 * chunk + f + 1)
                            act.sem_inc(s_carry2, 1)
                            act.activation(hT[:, c % 2, f, :], ps_s[:, f // 2, 512 * (f % 2):512 * (f % 2) + 512],
                                           ACT.Relu, bias=b1T[:, bass.ds(8 * q + 4 * w + f, 1)]).then_inc(relu_act, 1)
            act.wait_ge(s_var2, 3)
            act.activation(std[:], vareps[:], ACT.Sqrt).then_inc(s_std2, 1)

        @block.tensor
        def _(pe):
            pe.wait_ge(s_small, 64)
            pe.transpose(ps_m[:, 0:NE * FT], b1r[:], identf[0:NE * FT, 0:NE * FT]).then_inc(s_b1f, 1)
            pe.wait_ge(s_x2n, 1)
            for t in range(NT):
                last = pe.transpose(ps_s[:, t // 8, P * (t % 8):P * (t % 8) + P], xn[:, t, :], identf[:])
                if t % 4 == 3:
                    last.then_inc(s_tr, 1)
            for t in range(NT):
                pe.wait_ge(s_x2T, t // 4 + 1)
                last = pe.matmul(ps_r[:, 0, NE * t:NE * t + NE], xnT[:, P * t:P * t + P], rw[:], start=True, stop=True)
            last.then_inc(s_log, 1)
            pe.wait_ge(s_gate, 1)
            for t in range(NT):
                last = pe.transpose(ps_s[0:NE, t // 8, P * (t % 8):P * (t % 8) + P], gates[:, t, :], identf[:])
                if t % 4 == 3:
                    last.then_inc(s_gTf, 1)
            for c in range(NC):
                pe.wait_ge(s_gT, c + 1)
                if c >= 2:
                    pe.wait_ge(s_acc, c - 1)
                for t in range(4 * c, 4 * c + 4):
                    last = pe.matmul(ps_r[:, c % 2, P * (t % 4):P * (t % 4) + P], gT[:, P * t:P * t + P], b2[:],
                                     start=True, stop=True)
                last.then_inc(s_init, 1)
            pe.wait_ge(relu_dve, 2)
            pe.wait_ge(relu_act, 2)
            pe.matmul(ps_m[0:1, 0:1], identf[:, 0:1], identf[:, 0:1], start=True, stop=True).then_inc(s_y2, 2)
            pe.wait_ge(s_y2, 2)
            with pe.Fori(0, NE // 2) as q:
                for w in range(2):
                    pe.wait_ge(s_w12[w], 32 * q + 32)
                    for c in range(NC):
                        chunk = 8 * q + 4 * w + c
                        for f in range(FT):
                            pe.wait_ge(relu_dve if f % 2 else relu_act, 2 * chunk + f // 2 + 1)
                            pe.matmul(ps_s[:, f // 2, 512 * (f % 2):512 * (f % 2) + 512], w1[:, w, P * f:P * f + P],
                                      xnT[:, 512 * c:512 * c + 512], start=True, stop=True).then_inc(s_h, 1)
                        pe.wait_ge(relu_act, 2 * chunk + 4)
                        pe.wait_ge(relu_dve, 2 * chunk + 4)
                        pe.wait_ge(s_acc, chunk + NC - 1)
                        for t in range(4):
                            for f in range(FT):
                                last = pe.matmul(ps_m[:, 512 * (c % 2) + P * t:512 * (c % 2) + P * t + P],
                                                 hT[:, c % 2, f, P * t:P * t + P], w2[:, w, f, :],
                                                 start=f == 0, stop=f == FT - 1)
                        last.then_inc(s_y2, 1)


_INS = ['L0_attn_inputs', 'L0_attn_W_qkv', 'L0_attn_W_out', 'L0_ffn_router_W', 'L0_ffn_router_b', 'L0_ffn_W1',
        'L0_ffn_b1', 'L0_ffn_W2', 'L0_ffn_b2']
_OUTS = [((2, 1024, 128), 'float32')]


def kernel(**inputs):
    import numpy as _np
    import concourse.bacc as _bacc
    from concourse import mybir as _mybir
    from concourse.bass_utils import run_bass_kernel_spmd as _run

    nc = _bacc.Bacc("TRN2", target_bir_lowering=False, num_devices=1)
    arrays, args = {}, []
    for name in _INS:
        a = _np.ascontiguousarray(inputs[name])
        arrays[f"in_{name}_dram"] = a
        args.append(nc.dram_tensor(f"in_{name}_dram", a.shape, _mybir.dt.from_np(a.dtype), kind="ExternalInput").ap())
    for i, (shape, dtype) in enumerate(_OUTS):
        dt = _mybir.dt.from_np(_np.dtype(dtype))
        args.append(nc.dram_tensor(f"out_{i}_dram", shape, dt, kind="ExternalOutput").ap())
    build(nc, *args)
    r = _run(nc, [arrays], core_ids=[0])
    got = tuple(r.results[0][f"out_{i}_dram"] for i in range(len(_OUTS)))
    return got[0]
```

```python
from contextlib import ExitStack

import concourse.bass as bass
from concourse import mybir

F32 = mybir.dt.float32
F32R = mybir.dt.float32r
BF16 = mybir.dt.bfloat16
F16 = mybir.dt.float16
ALU = mybir.AluOpType
ACT = mybir.ActivationFunctionType
AX_X = mybir.AxisListType.X

P = 128
EPS = 1e-5
NEG = -1.0e30


def step_order(r, first, last):
    gone = set()
    if first and r == 0:
        gone |= {"O", "C"}
    if first and r == 1:
        gone |= {"T", "Y"}
    if last and r == 2:
        gone |= {"Q"}
    if last and r == 3:
        gone |= {"M", "R", "V"}
    even = "M0 M1 M2 Q0 M3 M4 Q1 M5 S0 C0 S1 Q2 M6 S2 M7 S3 Q3 M8 S4 S5 O0 S6 M9 S7 S8 M10 S9 M11 O1 B0 R0 S10 S11"
    odd = "M0 M1 T0 T1 M2 M3 Y0 M4 V0 M5 S0 S1 M6 V1 S2 M7 S3 S4 O0 S5 M8 M9 C0 S6 M10 Y1 S7 S8 M11 O1 S9 R0 S10 B0 S11"
    words = (odd if r % 2 else even).split()
    return [(w[0], int(w[1:])) for w in words if w[0] not in gone]


MAX_PIECES = [(i, c, min(512, P * (i + 1) - c)) for i in range(8) for c in range(0, P * (i + 1), 512)][::-1]
NM = len(MAX_PIECES)
SCORE_PIECES = [(j, c, min(512, P * (8 - j) - c)) for j in range(8) for c in range(0, P * (8 - j), 512)]
NS = len(SCORE_PIECES)
PIECES_UPTO = [sum(j < 4 * k + 4 for j, c, w in SCORE_PIECES) for k in range(2)]
RING_S = RING_M = 3

RING_KINDS = "OQVRTY"


def ring_counts(kind, i, r):
    return {
        "O": (8, 2 * (r - 1) + i + 1),
        "Q": (8, 4 * (r // 2 + 1) + i + 1),
        "V": (4, 2 * (r // 2 + 1) + i + 1),
        "R": (4, r + 2),
        "T": (4, 2 * (r // 2 - 1) + i + 1),
        "Y": (4, 2 * (r // 2 - 1) + i + 1),
    }[kind]


def ring_uses(first, last):
    return [((r, k, i), (k, *ring_counts(k, i, r))) for r in range(4) for k, i in step_order(r, first, last)
            if k in RING_KINDS]


def ring_plan():
    pro = [((0, "Q", i), ("Q", 0, i + 1)) for i in range(4)] + [((0, "V", i), ("V", 0, i + 1)) for i in range(2)]
    pro += [((0, "R", 0), ("R", 0, 1))]
    first, mid, last = ring_uses(True, False), ring_uses(False, False), ring_uses(False, True)
    epi = [((4, "O", k), ("O", 8, 6 + k + 1)) for k in range(2)]
    epi += [((5, k, c), (k, 4, 2 + c + 1)) for c in range(2) for k in "TY"]
    back = [(key, (k, a, c - a)) for key, (k, a, c) in mid]
    assert len(mid) % 2 == 0 and len(first) % 2 == 0
    plans = {}
    for name, before, uses, at in (("pro", [], pro, 1), ("first", pro, first, 0), ("mid", back, mid, 0),
                                   ("last", back, last, 0), ("epi", last, epi, len(last))):
        both = before + uses
        n0 = len(before)
        plans[name] = {
            key: ((at + n) % 2, both[n0 + n - 2][1] if n0 + n >= 2 else None) for n, (key, _) in enumerate(uses)
        }
    return plans


def build(nc, x_d, wqkv_d, wout_d, rw_d, rb_d, w1_d, b1_d, w2_d, b2_d, out_d):
    B, L, D = x_d.shape
    HD = wout_d.shape[0]
    DH = 64
    NPAIR = HD // P
    NE, _, F = w1_d.shape
    NT = B * L // P
    IT = L // P
    FT = F // P
    PW = (L + P) * IT // 2
    OFF = [(L + P) * j if j < IT // 2 else (L + P) * (IT - 1 - j) + P * (j + 1) for j in range(IT)]
    VC = DH + 1
    SCALE = DH ** -0.5
    assert B == 2 and IT == 8 and D == P and FT == 4 and NE == 8
    RING = ring_plan()

    with ExitStack() as ctx:
        def sb(name, shape, dt=F32):
            return ctx.enter_context(nc.sbuf_tensor(name, shape, dt))

        def sem(name):
            return ctx.enter_context(nc.semaphore(name))

        banks = ctx.enter_context(nc.psum_tensor("banks", [P, 8, 512], F32))
        ps_s, ps_m, ps_r = banks[:, 0:RING_S], banks[:, RING_S:RING_S + RING_M], banks[:, RING_S + RING_M:]

        x_sb = sb("x_sb", [P, NT, D])
        xn = sb("xn", [P, NT, D])
        xnT = sb("xnT", [P, NT * P])
        y_acc = sb("y_acc", [P, NT, D])
        identf = sb("identf", [P, P])
        mask_rows = sb("mask_rows", [P, 512])
        stats = sb("stats", [P, NT, 6])
        meanvar = sb("meanvar", [P, NT, 2])
        vareps = sb("vareps", [P, NT])
        std = sb("std", [P, NT])
        rstd = sb("rstd", [P, NT])

        s_x = sem("s_x")
        s_const = sem("s_const")
        s_pool = sem("s_pool")
        s_dve = sem("s_dve")
        s_var = sem("s_var")
        s_std = sem("s_std")
        s_xn = sem("s_xn")
        s_xt_full = sem("s_xt_full")
        s_xt = sem("s_xt")

        w_loaded = [sem(f"w_loaded{b}") for b in range(2)]
        s_wout = sem("s_wout")
        full = {k: sem(f"full_{k}") for k in "SMOQVRTY"}
        freed = {k: sem(f"freed_{k}") for k in "OQVRTY"}
        s_hi = sem("s_hi")
        s_q_stacked = sem("s_q_stacked")
        s_k_stacked = sem("s_k_stacked")
        s_v1 = sem("s_v1")
        s_max = sem("s_max")
        s_carry = sem("s_carry")
        s_carry_v = sem("s_carry_v")
        s_max_all = sem("s_max_all")
        s_mh = sem("s_mh")
        s_m_rows = sem("s_m_rows")
        s_exp = sem("s_exp")
        s_masked = sem("s_masked")
        s_plo = sem("s_plo")
        s_rec = sem("s_rec")

        SLOTS = NT + NE
        xs_d = nc.dram_tensor("xs_rows", [SLOTS * P, D], F32, kind="Internal").ap()
        ys_d = nc.dram_tensor("ys_rows", [SLOTS * P, D], F32, kind="Internal").ap()
        w1 = sb("w1", [P, NE, F])
        s_zeroed = sem("s_zeroed")
        s_w1 = sem("s_w1")

        main = ExitStack()
        with main:
            def sbm(name, shape, dt=F32):
                return main.enter_context(nc.sbuf_tensor(name, shape, dt))

            W = sbm("W", [P, 2, 3, P])
            wout = sbm("wout", [P, NPAIR * D])
            T1 = sbm("T1", [P, 2, 2, L], F32R)
            T2 = sbm("T2", [P, 2, 2, L], F32R)
            K1 = sbm("K1", [P, 2, 2, L], F32R)
            K2 = sbm("K2", [P, 2, 2, L], F32R)
            q_lo = sbm("q_lo", [P, L], F32R)
            v_hi = sbm("v_hi", [P, 2, IT, 2, VC + 1], BF16)
            v_lo = sbm("v_lo", [P, 2, IT, 2, DH], F16)
            probs = sbm("probs", [P, 2, PW])
            probs_lo = sbm("probs_lo", [P, 2, PW], F16)
            junk = sbm("junk", [P, RING_M, 512], BF16)
            mx_half = sbm("mx_half", [P, 2, 2, IT])
            mx = sbm("mx", [P, 2, IT])
            mh = sbm("mh", [IT, 2, P], F32R)
            ml = sbm("ml", [IT, 2, P], F32R)
            rec = sbm("rec", [P, IT])
            o_sb = sbm("o_sb", [P, 2, IT, P])
            oT = sbm("oT", [P, 2, 512])

            probs_hi = probs[:].bitcast(BF16).rearrange("p g (n t) -> p g n t", t=2)[:, :, :, 1]
            OWN = [(0, 64), (64, 128)]
            OTHER = [(64, 128), (0, 64)]

            def w_slice(p):
                return wqkv_d.rearrange("r (t p c) -> r t p c", t=3, p=NPAIR)[:, :, bass.ds(p, 1), :].rearrange(
                    "r t p c -> r t (p c)")

            block = main.enter_context(nc.Block())

            def run_bodies(eng, body):
                body(0, "first")
                with eng.Fori(1, NPAIR - 1) as p:
                    body(p, "mid")
                body(NPAIR - 1, "last")

            def stages(name):
                for r in range(4):
                    for kind, i in step_order(r, name == "first", name == "last"):
                        yield r, kind, i

            @block.sync
            def _(sp):
                sp.dma_start(x_sb[:], x_d.rearrange("b (t p) d -> p (b t) d", p=P)).then_inc(s_x, 16)
                for b in range(2):
                    sp.dma_start(W[:, b], w_slice(0)).then_inc(w_loaded[b], 16)
                sp.dma_start(wout[:].rearrange("r (p n) -> r p n", n=D),
                             wout_d.rearrange("(p r) n -> r p n", r=P)).then_inc(s_wout, 16)

                def stack_q(u, b):
                    sp.wait_ge(freed["Q"], 4 * u + 2)
                    for s in range(2):
                        (o0, o1), (t0, t1) = OWN[s], OTHER[s]
                        sp.dma_start(T1[t0:t1, b, s, :].bitcast(F32), q_lo[o0:o1, :].bitcast(F32)).then_inc(s_q_stacked, 16)
                        sp.dma_start(T2[o0:o1, b, s, :].bitcast(F32), T1[o0:o1, b, s, :].bitcast(F32)).then_inc(s_q_stacked, 16)

                def stack_k(u, b):
                    sp.wait_ge(freed["Q"], 4 * u + 4)
                    for s in range(2):
                        (o0, o1), (t0, t1) = OWN[s], OTHER[s]
                        sp.dma_start(K1[t0:t1, b, s, :].bitcast(F32), K1[o0:o1, b, s, :].bitcast(F32)).then_inc(s_k_stacked, 16)

                def max_rows(g, b, s):
                    t0 = OTHER[s][0]
                    for n, (part, ready) in enumerate(((mh, s_mh), (ml, freed["R"]))):
                        sp.wait_ge(ready, g + 1)
                        sp.dma_start(T2[t0 + n:t0 + n + 1, b, s, :].bitcast(F32).rearrange(
                            "o (t i) -> o t i", i=P), part[:, s, :].bitcast(F32)).then_inc(s_m_rows, 16)

                sp.wait_ge(s_const, 8)
                xs_flat = xs_d.rearrange("(q k) d -> q (k d)", q=P)
                for c0 in range(0, SLOTS * D, NT * D):
                    c1 = min(SLOTS * D, c0 + NT * D)
                    sp.dma_start(xs_flat[:, c0:c1], y_acc[:].rearrange("q t d -> q (t d)")[:, 0:c1 - c0]
                                 ).then_inc(s_zeroed, 16)
                stack_q(0, 0)
                stack_k(0, 0)
                max_rows(0, 0, 0)
                sp.dma_start(w1[:], w1_d.rearrange("e r f -> r e f")).then_inc(s_w1, 16)

                def body(p, name):
                    for r, kind, i in stages(name):
                        u1 = 2 * p + r // 2 + 1
                        b1 = (r // 2 + 1) % 2
                        if r in (0, 2) and (kind, i) == ("S", 0) and name != "last":
                            b = r // 2
                            sp.wait_ge(full["V"], 4 * p + 2 * b + 2)
                            sp.dma_start(W[:, b], w_slice(p + 1)).then_inc(w_loaded[b], 16)
                        if (kind, i) == ("Q", 1):
                            stack_q(u1, b1)
                        if (kind, i) == ("Q", 3):
                            stack_k(u1, b1)
                        if kind == "R":
                            max_rows(4 * p + r + 1, (r + 1) // 2 % 2, (r + 1) % 2)

                run_bodies(sp, body)

            @block.gpsimd
            def _(pool):
                n = [0]

                def link(ins):
                    n[0] += 1
                    ins.then_inc(s_pool, 1)
                    pool.wait_ge(s_pool, n[0])

                link(pool.memset(identf[:], 0.0))
                pool.affine_select(out=identf[:], in_=identf[:], compare_op=ALU.not_equal, fill=1.0, base=0,
                                   pattern=[[-1, P]], channel_multiplier=1).then_inc(s_const, 1)
                pool.memset(T2[:].bitcast(F32), 0.0).then_inc(s_const, 1)
                pool.memset(y_acc[:], 0.0).then_inc(s_const, 1)
                link(pool.memset(K2[:].bitcast(F32), 0.0))
                for s in range(2):
                    t0 = OTHER[s][0]
                    pool.memset(K2[t0:t0 + 2, :, s, :].bitcast(F32), 1.0).then_inc(s_const, 1)
                    pool.wait_ge(s_const, 4 + s)
                pool.memset(mx_half[:], -3.0e38).then_inc(s_const, 1)
                link(pool.memset(mask_rows[:], 0.0))
                pool.affine_select(out=mask_rows[:, 512 - P:], in_=mask_rows[:, 512 - P:], compare_op=ALU.is_ge, fill=NEG,
                                   base=0, pattern=[[-1, P]], channel_multiplier=1).then_inc(s_const, 1)
                pool.memset(v_hi[:, :, :, :, DH:], 1.0).then_inc(s_const, 1)

                def p_low(g, s, k):
                    pool.wait_ge(s_exp, NS * g + PIECES_UPTO[k])
                    pool.sem_inc(s_carry, 1)
                    if k == 0:
                        blocks = probs[:, s, :].rearrange("q (j c) -> q j c", c=L + P)[:, :, 0:P]
                    else:
                        blocks = probs[:, s, L // 2:].rearrange("q (j c) -> q j c", c=L)[:, :, L // 2:L // 2 + P]
                    pool.affine_select(out=blocks, in_=blocks, compare_op=ALU.is_ge, fill=0.0, base=0,
                                       pattern=[[0, 4], [1, P]], channel_multiplier=-1).then_inc(s_masked, 1)
                    pool.wait_ge(s_masked, 2 * g + k + 1)
                    for j in range(4 * k, 4 * k + 4):
                        part = slice(OFF[j], OFF[j] + L - P * j)
                        pool.tensor_tensor(probs_lo[:, s, part], probs[:, s, part], probs_hi[:, s, part],
                                           ALU.subtract).then_inc(s_plo, 1)

                def body(p, name):
                    for r, kind, i in stages(name):
                        if kind == "B":
                            p_low(4 * p + r, r % 2, 0)
                        if kind == "C":
                            p_low(4 * p + r - 1, (r - 1) % 2, 1)

                run_bodies(pool, body)
                p_low(4 * NPAIR - 1, 1, 1)

            @block.vector
            def _(dve):
                n = [0]

                def link(ins):
                    n[0] += 1
                    ins.then_inc(s_dve, 1)
                    dve.wait_ge(s_dve, n[0])

                dve.wait_ge(s_x, 16)
                for t in range(NT):
                    last = dve.bn_stats(stats[:, t, :], x_sb[:, t, :])
                link(last)
                for t in range(NT):
                    last = dve.bn_aggr(meanvar[:, t, :], stats[:, t, :])
                link(last)
                dve.tensor_scalar(vareps[:], meanvar[:, :, 1], EPS, None, ALU.add).then_inc(s_var, 1)
                dve.wait_ge(s_std, 1)
                link(dve.reciprocal(rstd[:], std[:]))
                for t in range(NT):
                    dve.tensor_scalar(xn[:, t, :], x_sb[:, t, :], meanvar[:, t, 0:1], rstd[:, t:t + 1],
                                      ALU.subtract, ALU.mult).then_inc(s_xn, 1)
                for c in range(0, 4):
                    dve.wait_ge(s_xt_full, 4 * c + 4)
                    dve.tensor_copy(xnT[:, 512 * c:512 * c + 512], banks[:, c, :]).then_inc(s_xt, 1)

                dve.wait_ge(s_const, 8)
                dve.wait_ge(s_zeroed, 32)

                def q_low(u, b, i, bank):
                    dve.wait_ge(s_hi, 4 * u + i + 1)
                    c = 512 * (i % 2)
                    for s in range(2):
                        o0, o1 = OWN[s]
                        hi = (T1 if i < 2 else K1)[o0:o1, b, s, c:c + 512].bitcast(F32)
                        dst = q_lo[o0:o1, c:c + 512] if i < 2 else K2[o0:o1, b, s, c:c + 512]
                        last = dve.tensor_tensor(dst, ps_r[o0:o1, bank, :], hi, ALU.subtract)
                    last.then_inc(freed["Q"], 1)

                def v_low(u, b, i, bank):
                    dve.wait_ge(s_v1, 2 * u + i + 1)
                    dve.tensor_tensor(v_lo[:, b, 4 * i:4 * i + 4, :, :],
                                      ps_r[:, bank, :].rearrange("p (t s d) -> p t s d", t=4, s=2),
                                      v_hi[:, b, 4 * i:4 * i + 4, :, 0:DH], ALU.subtract).then_inc(freed["V"], 1)

                def row_max(g, s, n):
                    i, c, w = MAX_PIECES[n]
                    dve.wait_ge(full["M"], NM * g + n + 1)
                    dst = mx_half[:, s, c // 512, i:i + 1]
                    if c + w == P * (i + 1):
                        dve.sem_inc(s_carry_v, 1)
                        dve.tensor_tensor_reduce(junk[:, n % RING_M, 0:w], ps_m[:, n % RING_M, 0:w], mask_rows[:, 512 - w:], 1.0,
                                                 -3.0e38, ALU.add, ALU.max, dst).then_inc(s_max, 1)
                    else:
                        dve.tensor_reduce(dst, ps_m[:, n % RING_M, 0:w], AX_X, ALU.max).then_inc(s_max, 1)
                    if n == NM - 1:
                        dve.wait_ge(s_max, NM * g + NM)
                        dve.tensor_tensor(mx[:, s, :], mx_half[:, s, 0, :], mx_half[:, s, 1, :], ALU.max
                                          ).then_inc(s_max_all, 1)

                def max_split(g, s, bank):
                    dve.wait_ge(full["R"], g + 1)
                    dve.tensor_scalar(mh[:, s, :], ps_r[0:IT, bank, 0:P], -1.0, None, ALU.mult).then_inc(s_mh, 1)
                    dve.wait_ge(s_mh, g + 1)
                    dve.scalar_tensor_tensor(ml[:, s, :], ps_r[0:IT, bank, 0:P], -1.0, mh[:, s, :].bitcast(F32),
                                             ALU.mult, ALU.subtract).then_inc(freed["R"], 1)

                def normalise(g, b, s, k, bank):
                    dve.wait_ge(full["O"], 2 * g + k + 1)
                    four = ps_r[:, bank, 0:4 * VC].rearrange("p (t c) -> p t c", t=4)
                    dve.reciprocal(rec[:, 4 * k:4 * k + 4], four[:, :, DH]).then_inc(s_rec, 1)
                    dve.wait_ge(s_rec, 2 * g + k + 1)
                    dve.tensor_tensor(o_sb[:, b, 4 * k:4 * k + 4, DH * s:DH * s + DH], four[:, :, 0:DH],
                                      rec[:, 4 * k:4 * k + 4].unsqueeze(2).to_broadcast([P, 4, DH]),
                                      ALU.mult).then_inc(freed["O"], 1)

                def accumulate(u, b, c, bank):
                    dve.wait_ge(full["Y"], 2 * u + c + 1)
                    ya = y_acc[:, IT * b + 4 * c:IT * b + 4 * c + 4, :]
                    dve.tensor_tensor(ya, ps_r[:, bank, :].rearrange("p (t d) -> p t d", t=4), ya,
                                      ALU.add).then_inc(freed["Y"], 1)

                for i in range(4):
                    q_low(0, 0, i, RING["pro"][(0, "Q", i)][0])
                for i in range(2):
                    v_low(0, 0, i, RING["pro"][(0, "V", i)][0])
                for i in range(NM):
                    row_max(0, 0, i)
                max_split(0, 0, RING["pro"][(0, "R", 0)][0])

                def body(p, name):
                    for r, kind, i in stages(name):
                        g = 4 * p + r
                        u1, b1 = 2 * p + r // 2 + 1, (r // 2 + 1) % 2
                        bank = RING[name][(r, kind, i)][0] if kind in RING_KINDS else None
                        if kind == "M":
                            if i == 0 and not (name == "first" and r == 0):
                                dve.wait_ge(full["R"], g)
                            row_max(g + 1, (r + 1) % 2, i)
                        if kind == "R":
                            if not (name == "first" and r == 0):
                                dve.wait_ge(s_m_rows, 32 * g)
                            max_split(g + 1, (r + 1) % 2, bank)
                        if kind == "O":
                            normalise(g - 1, (r - 1) // 2 % 2, (r - 1) % 2, i, bank)
                        if kind == "Q":
                            if i == 0:
                                dve.wait_ge(s_q_stacked, 64 * u1)
                            q_low(u1, b1, i, bank)
                        if kind == "V":
                            v_low(u1, b1, i, bank)
                        if kind == "Y":
                            accumulate(u1 - 2, b1, i, bank)

                run_bodies(dve, body)
                for k in range(2):
                    normalise(4 * NPAIR - 1, 1, 1, k, RING["epi"][(4, "O", k)][0])
                for c in range(2):
                    accumulate(2 * NPAIR - 1, 1, c, RING["epi"][(5, "Y", c)][0])

            @block.scalar
            def _(act):
                act.wait_ge(s_var, 1)
                act.activation(std[:], vareps[:], ACT.Sqrt).then_inc(s_std, 1)

                def q_high(u, b, i, bank):
                    act.wait_ge(full["Q"], 4 * u + i + 1)
                    c = 512 * (i % 2)
                    for s in range(2):
                        o0, o1 = OWN[s]
                        last = act.activation((T1 if i < 2 else K1)[o0:o1, b, s, c:c + 512], ps_r[o0:o1, bank, :],
                                              ACT.Copy)
                    last.then_inc(s_hi, 1)

                def v_high(u, b, i, bank):
                    act.wait_ge(full["V"], 2 * u + i + 1)
                    act.activation(v_hi[:, b, 4 * i:4 * i + 4, :, 0:DH],
                                   ps_r[:, bank, :].rearrange("p (t s d) -> p t s d", t=4, s=2),
                                   ACT.Copy).then_inc(s_v1, 1)

                def exps(g, s, n):
                    j, c, w = SCORE_PIECES[n]
                    act.wait_ge(full["S"], NS * g + n + 1)
                    act.activation(probs[:, s, OFF[j] + c:OFF[j] + c + w], ps_s[:, n % RING_S, 0:w], ACT.Exp,
                                   scale=SCALE).then_inc(s_exp, 1)

                def o_turned(u, c, bank):
                    act.wait_ge(full["T"], 2 * u + c + 1)
                    act.activation(oT[:, c, :], ps_r[:, bank, :], ACT.Copy).then_inc(freed["T"], 1)

                for i in range(4):
                    q_high(0, 0, i, RING["pro"][(0, "Q", i)][0])
                for i in range(2):
                    v_high(0, 0, i, RING["pro"][(0, "V", i)][0])

                def body(p, name):
                    for r, kind, i in stages(name):
                        g = 4 * p + r
                        u1, b1 = 2 * p + r // 2 + 1, (r // 2 + 1) % 2
                        bank = RING[name][(r, kind, i)][0] if kind in RING_KINDS else None
                        if kind == "S":
                            if i == 0 and not (name == "first" and r < 2):
                                act.wait_ge(full["O"], 2 * g - 2)
                            exps(g, r % 2, i)
                        if kind == "Q":
                            q_high(u1, b1, i, bank)
                        if kind == "V":
                            v_high(u1, b1, i, bank)
                        if kind == "T":
                            o_turned(u1 - 2, i, bank)

                run_bodies(act, body)
                for c in range(2):
                    o_turned(2 * NPAIR - 1, c, RING["epi"][(5, "T", c)][0])

            @block.tensor
            def _(pe):
                def wait_bank(use, p):
                    if use is not None:
                        kind, a, c = use
                        pe.wait_ge(freed[kind], a * p + c)

                def project(u, b, i, bank):
                    if i == 0:
                        pe.wait_ge(w_loaded[b], 16 * (u // 2 + 1) if isinstance(u, int) else 8 * u + (16 if b == 0 else 8))
                    t = i // 2
                    tok = L * b + 512 * (i % 2)
                    pe.matmul(ps_r[:, bank, :], W[:, b, t, :], xnT[:, tok:tok + 512], start=True, stop=True
                              ).then_inc(full["Q"], 1)

                def values(u, b, i, bank):
                    for t in range(4):
                        tok = L * b + P * (4 * i + t)
                        last = pe.matmul(ps_r[:, bank, P * t:P * t + P], xnT[:, tok:tok + P], W[:, b, 2, :],
                                         start=True, stop=True)
                    last.then_inc(full["V"], 1)

                def max_scores(g, u, b, s, n):
                    if n == 0:
                        pe.wait_ge(s_q_stacked, 64 * u + 64)
                        pe.wait_ge(s_k_stacked, 32 * u + 32)
                    i, c, w = MAX_PIECES[n]
                    pe.matmul(ps_m[:, n % RING_M, 0:w], T1[:, b, s, P * i:P * i + P], K1[:, b, s, c:c + w],
                              start=True, stop=True).then_inc(full["M"], 1)

                def max_turned(g, s, bank):
                    pe.wait_ge(s_max_all, g + 1)
                    pe.transpose(ps_r[0:IT, bank, 0:P], mx[:, s, :], identf[:]).then_inc(full["R"], 1)

                def scores(g, b, s, n):
                    if n == 0:
                        pe.wait_ge(s_m_rows, 32 * g + 32)
                    j, c, w = SCORE_PIECES[n]
                    rows = slice(P * j + c, P * j + c + w)
                    pe.matmul(ps_s[:, n % RING_S, 0:w], K1[:, b, s, P * j:P * j + P], T1[:, b, s, rows],
                              start=True, stop=False)
                    pe.matmul(ps_s[:, n % RING_S, 0:w], K2[:, b, s, P * j:P * j + P], T2[:, b, s, rows],
                              start=False, stop=True).then_inc(full["S"], 1)

                def value_products(g, b, s, k, bank):
                    pe.wait_ge(s_plo, 8 * g + 4 * k + 4)
                    for e in range(4):
                        it = 4 * k + e
                        dst = ps_r[:, bank, VC * e:VC * e + VC]
                        for j in range(it + 1):
                            at = OFF[j] + P * (it - j)
                            hi, lo = probs_hi[:, s, at:at + P], probs_lo[:, s, at:at + P]
                            pe.matmul(dst, hi, v_hi[:, b, j, s, 0:VC], start=j == 0, stop=False,
                                      skip_group_check=True)
                            pe.matmul(dst[:, 0:DH], hi, v_lo[:, b, j, s, :], start=False, stop=False,
                                      skip_group_check=True)
                            last = pe.matmul(dst, lo, v_hi[:, b, j, s, 0:VC], start=False, stop=j == it,
                                             skip_group_check=True)
                    last.then_inc(full["O"], 1)

                def turn_outputs(u, b, c, bank):
                    pe.wait_ge(freed["O"], 4 * u + 2 + c + 1)
                    for t in range(4):
                        last = pe.transpose(ps_r[:, bank, P * t:P * t + P], o_sb[:, b, 4 * c + t, :], identf[:])
                    last.then_inc(full["T"], 1)

                def out_project(u, b, c, p, bank):
                    pe.wait_ge(freed["T"], 2 * u + c + 1)
                    for t in range(4):
                        last = pe.matmul(ps_r[:, bank, P * t:P * t + P], oT[:, c, P * t:P * t + P],
                                         wout[:, bass.ts(p, D)], start=True, stop=True)
                    last.then_inc(full["Y"], 1)

                pe.wait_ge(s_const, 8)
                for t in range(NT):
                    pe.wait_ge(s_xn, t + 1)
                    pe.transpose(banks[:, t // 4, P * (t % 4):P * (t % 4) + P], xn[:, t, :], identf[:]
                                 ).then_inc(s_xt_full, 1)
                pe.wait_ge(s_xt, 4)
                for i in range(4):
                    bank, use = RING["pro"][(0, "Q", i)]
                    wait_bank(use, 0)
                    project(0, 0, i, bank)
                for i in range(2):
                    bank, use = RING["pro"][(0, "V", i)]
                    wait_bank(use, 0)
                    values(0, 0, i, bank)
                for i in range(NM):
                    if i >= RING_M:
                        pe.wait_ge(s_max, i - RING_M + 1)
                    max_scores(0, 0, 0, 0, i)
                bank, use = RING["pro"][(0, "R", 0)]
                wait_bank(use, 0)
                max_turned(0, 0, bank)
                pe.wait_ge(s_wout, 16)

                def body(p, name):
                    for r, kind, i in stages(name):
                        g = 4 * p + r
                        u1, b1 = 2 * p + r // 2 + 1, (r // 2 + 1) % 2
                        if kind in RING_KINDS:
                            bank, use = RING[name][(r, kind, i)]
                            wait_bank(use, p)
                        if kind == "S":
                            if not (name == "first" and r == 0 and i < RING_S):
                                pe.wait_ge(s_exp, NS * g + i - RING_S + 1)
                            scores(g, (r // 2) % 2, r % 2, i)
                        if kind == "M":
                            pe.wait_ge(s_max, NM * (g + 1) + i - RING_M + 1)
                            max_scores(g + 1, 2 * p + (r + 1) // 2, (r + 1) // 2 % 2, (r + 1) % 2, i)
                        if kind == "R":
                            max_turned(g + 1, (r + 1) % 2, bank)
                        if kind == "O":
                            if i == 0 and (r - 1) % 2 == 0:
                                pe.wait_ge(freed["V"], 2 * (2 * p + (r - 1) // 2) + 2)
                            value_products(g - 1, (r - 1) // 2 % 2, (r - 1) % 2, i, bank)
                        if kind == "Q":
                            project(u1, b1, i, bank)
                        if kind == "V":
                            values(u1, b1, i, bank)
                        if kind == "T":
                            turn_outputs(u1 - 2, b1, i, bank)
                        if kind == "Y":
                            out_project(u1 - 2, b1, i, p - 1 if r == 1 else p, bank)

                run_bodies(pe, body)
                for k in range(2):
                    bank, use = RING["epi"][(4, "O", k)]
                    wait_bank(use, NPAIR - 1)
                    value_products(4 * NPAIR - 1, 1, 1, k, bank)
                for c in range(2):
                    bank, use = RING["epi"][(5, "T", c)]
                    wait_bank(use, NPAIR - 1)
                    turn_outputs(2 * NPAIR - 1, 1, c, bank)
                    bank, use = RING["epi"][(5, "Y", c)]
                    wait_bank(use, NPAIR - 1)
                    out_project(2 * NPAIR - 1, 1, c, NPAIR - 1, bank)

        moe(nc, ctx, sb, sem, x_sb, xn, xnT, y_acc, identf, stats, meanvar, vareps, std, rstd, banks,
            rw_d, rb_d, w1, s_w1, b1_d, w2_d, b2_d, out_d, xs_d, ys_d, SLOTS, NT, D, NE, F, FT)


def moe(nc, ctx, sb, sem, x_sb, xn, xnT, acc, identf, stats, meanvar, vareps, std, rstd, banks,
        rw_d, rb_d, w1, s_w1, b1_d, w2_d, b2_d, out_d, xs_d, ys_d, SLOTS, NT, D, NE, F, FT):
    BODY = 4
    ps_m, ps_r = banks[:, 4:6], banks[:, 6:8]
    assert SLOTS % BODY == 0
    NC = NT // 4
    w2 = sb("w2", [P, NE, FT, D])
    b1_rows = sb("b1_rows", [P, NE, F])
    b2_rows = sb("b2_rows", [P, NE, D])
    rw = sb("rw", [P, NE])
    rb = sb("rb", [P, NE])
    logits = sb("logits", [P, NT, NE])
    exps = sb("exps", [P, NT, NE])
    top1 = sb("top1", [P, NT, NE])
    top1_b = sb("top1_b", [P, NT * NE], BF16)
    ones_b = sb("ones_b", [P, P], BF16)
    before_b = sb("before_b", [P, P], BF16)
    falling = sb("falling", [P, NE])
    tile_no = sb("tile_no", [P, SLOTS])
    top_logit = sb("top_logit", [P, NT])
    den = sb("den", [P, NT])
    ptop = sb("ptop", [P, NT])
    count_i = sb("count_i", [P, NE], mybir.dt.int32)
    tiles_i = sb("tiles_i", [P, NE], mybir.dt.int32)
    ends = sb("ends", [P, 4, NE + 4])
    start = sb("start", [P, NE])
    place = sb("place", [P, NT, NE])
    slot_f = sb("slot_f", [P, NT])
    slot = sb("slot", [P, NT], mybir.dt.uint32)
    passed = sb("passed", [P, SLOTS, NE])
    expert_f = sb("expert_f", [P, SLOTS])
    expert = sb("expert", [P, SLOTS], mybir.dt.int32)
    xs = sb("xs", [P, BODY, D])
    xsT = sb("xsT", [P, BODY * P])
    h = sb("h", [P, BODY, F])
    hT = sb("hT", [P, 2, F])
    ys = sb("ys", [P, BODY, D])

    s_small = sem("s_small")
    s_big = sem("s_big")
    s_c2 = sem("s_c2")
    s_cc = sem("s_cc")
    s_d = sem("s_d")
    s_var2 = sem("s_var2")
    s_std2 = sem("s_std2")
    s_x2n = sem("s_x2n")
    s_tr = sem("s_tr")
    s_x2T = sem("s_x2T")
    s_log = sem("s_log")
    s_dif = sem("s_dif")
    s_ex = sem("s_ex")
    s_top1 = sem("s_top1")
    s_rank = sem("s_rank")
    s_slot = sem("s_slot")
    s_expert = sem("s_expert")
    s_scattered = sem("s_scattered")
    s_xs = sem("s_xs")
    full_x = sem("full_x")
    s_xsT = sem("s_xsT")
    full_h = sem("full_h")
    s_h = sem("s_h")
    full_hT = sem("full_hT")
    s_hT = sem("s_hT")
    full_y = sem("full_y")
    s_y = sem("s_y")
    s_stored = sem("s_stored")
    s_back = [sem(f"s_back{c}") for c in range(NC)]
    s_res = sem("s_res")
    s_out = sem("s_out")

    ORDER = "A0 A1 A2 B0 A3 B1 X0 C0 B2 C1 B3 C2 C3".split()
    NB = SLOTS // BODY

    def run_bodies(eng, body):
        with eng.Fori(0, NB - 1) as q:
            body(q, False)
        body(NB - 1, True)

    with nc.Block() as block:
        @block.sync
        def _(sp):
            sp.dma_start(rw[:], rw_d).then_inc(s_small, 16)
            sp.dma_start(rb[:], rb_d.partition_broadcast(P)).then_inc(s_small, 16)
            sp.dma_start(w2[:], w2_d.rearrange("e (f q) d -> q e f d", q=P)).then_inc(s_big, 16)
            sp.dma_start(b1_rows[:], b1_d.partition_broadcast(P)).then_inc(s_big, 16)
            sp.dma_start(b2_rows[:], b2_d.partition_broadcast(P)).then_inc(s_big, 16)

            def fetch(q):
                sp.dma_start(xs[:], xs_d.rearrange("(b k p) d -> b p k d", p=P, k=BODY)[bass.ds(q, 1)].rearrange(
                    "b p k d -> p (b k) d")).then_inc(s_xs, 16)

            def store(q):
                sp.wait_ge(s_y, BODY * q + BODY)
                sp.dma_start(ys_d.rearrange("(b k p) d -> b p k d", p=P, k=BODY)[bass.ds(q, 1)].rearrange(
                    "b p k d -> p (b k) d"), ys[:]).then_inc(s_stored, 16)

            sp.wait_ge(s_scattered, 16 * NT)
            fetch(0)
            sp.wait_ge(full_x, 1)
            fetch(1)
            with sp.Fori(0, NB - 2) as q:
                sp.wait_ge(full_x, q + 2)
                fetch(q + 2)
                store(q)
            for q in range(NB - 2, NB):
                store(q)
            for c in range(NC):
                sp.wait_ge(s_res, c + 1)
                sp.dma_start(out_d.rearrange("b (t p) d -> p (b t) d", p=P)[:, 4 * c:4 * c + 4, :],
                             x_sb[:, 4 * c:4 * c + 4, :]).then_inc(s_out, 16)
            sp.wait_ge(s_out, 16 * NC)

        @block.gpsimd
        def _(pool):
            pool.iota(falling[:], [[-1, NE]], base=NE, channel_multiplier=0,
                      allow_small_or_imprecise_dtypes=True).then_inc(s_c2, 1)
            pool.iota(tile_no[:], [[1, SLOTS]], base=0, channel_multiplier=0,
                      allow_small_or_imprecise_dtypes=True).then_inc(s_c2, 1)
            pool.memset(ends[:], 0.0).then_inc(s_c2, 1)
            pool.memset(ones_b[:], 1.0).then_inc(s_c2, 1)
            pool.wait_ge(s_c2, 4)
            pool.affine_select(out=before_b[:], in_=ones_b[:], compare_op=ALU.is_gt, fill=0.0, base=0,
                               pattern=[[1, P]], channel_multiplier=-1).then_inc(s_c2, 1)
            pool.wait_ge(s_slot, 1)
            for t in range(NT):
                pool.indirect_dma_start(xs_d, bass.IndirectOffsetOnAxis(ap=slot[:, t:t + 1], axis=0), xn[:, t, :],
                                        None).then_inc(s_scattered, 16)
            pool.wait_ge(s_stored, 16 * NB)
            for t in range(NT):
                pool.indirect_dma_start(acc[:, t, :], None, ys_d,
                                        bass.IndirectOffsetOnAxis(ap=slot[:, t:t + 1], axis=0)
                                        ).then_inc(s_back[t // 4], 16)

        @block.vector
        def _(dve):
            n = [0]

            def link(ins):
                n[0] += 1
                ins.then_inc(s_d, 1)
                dve.wait_ge(s_d, n[0])

            def statistics(src, ts):
                for t in ts:
                    last = dve.bn_stats(stats[:, t, :], src[:, t, :])
                link(last)
                for t in ts:
                    last = dve.bn_aggr(meanvar[:, t, :], stats[:, t, :])
                link(last)

            def normalise(src, dst, k):
                statistics(src, range(NT))
                dve.tensor_scalar(vareps[:], meanvar[:, :, 1], EPS, None, ALU.add).then_inc(s_var2, 1)
                dve.wait_ge(s_std2, k)
                link(dve.reciprocal(rstd[:], std[:]))
                for t in range(NT):
                    last = dve.tensor_scalar(dst[:, t, :], src[:, t, :], meanvar[:, t, 0:1], rstd[:, t:t + 1],
                                             ALU.subtract, ALU.mult)
                return last

            link(normalise(acc, xn, 1))
            link(dve.tensor_tensor(x_sb[:], x_sb[:], xn[:], ALU.add))
            normalise(x_sb, xn, 2).then_inc(s_x2n, 1)
            for c in range(NC):
                dve.wait_ge(s_tr, c + 1)
                dve.tensor_copy(xnT[:, 512 * c:512 * c + 512], banks[:, c, :]).then_inc(s_x2T, 1)
            dve.wait_ge(s_log, 1)
            dve.wait_ge(s_small, 32)
            dve.wait_ge(s_c2, 5)
            link(dve.tensor_tensor(logits[:], ps_r[:, 0, 0:NT * NE].rearrange("p (t e) -> p t e", e=NE),
                                   rb[:].unsqueeze(1).to_broadcast([P, NT, NE]), ALU.add))
            link(dve.tensor_reduce(top_logit[:], logits[:], AX_X, ALU.max))
            dve.tensor_tensor(logits[:], logits[:], top_logit[:].unsqueeze(2).to_broadcast([P, NT, NE]), ALU.subtract
                              ).then_inc(s_dif, 1)
            dve.wait_ge(s_dif, 1)
            link(dve.tensor_scalar(top1[:], logits[:], 0.0, None, ALU.is_ge))
            link(dve.tensor_tensor(top1[:], top1[:], falling[:].unsqueeze(1).to_broadcast([P, NT, NE]), ALU.mult))
            link(dve.tensor_reduce(top_logit[:], top1[:], AX_X, ALU.max))
            link(dve.tensor_tensor(top1[:], top1[:], top_logit[:].unsqueeze(2).to_broadcast([P, NT, NE]),
                                   ALU.is_equal))
            dve.tensor_copy(top1_b[:], top1[:].rearrange("p t e -> p (t e)")).then_inc(s_top1, 1)
            dve.wait_ge(s_ex, 1)
            link(dve.tensor_reduce(den[:], exps[:], AX_X, ALU.add))
            link(dve.reciprocal(ptop[:], den[:]))
            dve.wait_ge(s_rank, 1)
            link(dve.tensor_scalar(count_i[:], ps_m[:, 0, NT * NE:NT * NE + NE], float(P - 1), None, ALU.add))
            link(dve.tensor_scalar(tiles_i[:], count_i[:], P.bit_length() - 1, None, ALU.logical_shift_right))
            link(dve.tensor_copy(ends[:, 0, 4:], tiles_i[:]))
            for k in range(3):
                sh = 1 << k
                link(dve.tensor_tensor(ends[:, k + 1, 4:], ends[:, k, 4:], ends[:, k, 4 - sh:4 - sh + NE], ALU.add))
            end = ends[:, 3, 4:]
            link(dve.tensor_tensor(start[:], end, ends[:, 0, 4:], ALU.subtract))
            link(dve.tensor_scalar(start[:], start[:], float(P), None, ALU.mult))
            link(dve.tensor_tensor(place[:], ps_m[:, 0, 0:NT * NE].rearrange("p (t e) -> p t e", e=NE),
                                   start[:].unsqueeze(1).to_broadcast([P, NT, NE]), ALU.add))
            link(dve.tensor_tensor(place[:], place[:], top1[:], ALU.mult))
            link(dve.tensor_reduce(slot_f[:], place[:], AX_X, ALU.add))
            dve.tensor_copy(slot[:], slot_f[:]).then_inc(s_slot, 1)
            link(dve.tensor_tensor(passed[:], tile_no[:].unsqueeze(2).to_broadcast([P, SLOTS, NE]),
                                   end.unsqueeze(1).to_broadcast([P, SLOTS, NE]), ALU.is_ge))
            link(dve.tensor_reduce(expert_f[:], passed[:], AX_X, ALU.add))
            dve.tensor_scalar(expert[:], expert_f[:], float(NE - 1), None, ALU.min).then_inc(s_expert, 1)
            dve.wait_ge(s_expert, 1)
            dve.wait_ge(s_big, 48)

            def body(q, last_body):
                es = []
                for word in ORDER:
                    kind, k = word[0], int(word[1])
                    if kind == "A":
                        j = BODY * q + k
                        e = dve.value_load(expert[0:1, bass.ds(j, 1)], min_val=0, max_val=NE - 1)
                        es.append(e)
                        dve.wait_ge(full_h, j + 1)
                        dve.tensor_tensor(h[:, k, :], banks[:, k, :],
                                          b1_rows[:, bass.ds(e, 1), :].rearrange("p e f -> p (e f)"), ALU.add
                                          ).then_inc(s_h, 1)
                dve.wait_ge(s_stored, 16 * q)
                dve.wait_ge(full_y, q + 1)
                for k in range(BODY):
                    dve.tensor_tensor(ys[:, k, :], ps_r[:, 1, P * k:P * k + P],
                                      b2_rows[:, bass.ds(es[k], 1), :].rearrange("p e d -> p (e d)"), ALU.add
                                      ).then_inc(s_y, 1)

            run_bodies(dve, body)
            for c in range(NC):
                ts = slice(4 * c, 4 * c + 4)
                dve.wait_ge(s_back[c], 64)
                statistics(acc, range(4 * c, 4 * c + 4))
                link(dve.tensor_tensor(vareps[:, ts], meanvar[:, ts, 1], ptop[:, ts], ALU.mult))
                link(dve.tensor_tensor(vareps[:, ts], vareps[:, ts], ptop[:, ts], ALU.mult))
                link(dve.tensor_scalar(vareps[:, ts], vareps[:, ts], EPS, None, ALU.add))
                dve.tensor_copy(den[:, ts], vareps[:, ts]).then_inc(s_var2, 1)
                dve.wait_ge(s_std2, 3 + c)
                link(dve.reciprocal(rstd[:, ts], std[:, ts]))
                link(dve.tensor_tensor(rstd[:, ts], rstd[:, ts], ptop[:, ts], ALU.mult))
                for t in range(4 * c, 4 * c + 4):
                    last = dve.tensor_scalar(acc[:, t, :], acc[:, t, :], meanvar[:, t, 0:1], rstd[:, t:t + 1],
                                             ALU.subtract, ALU.mult)
                link(last)
                dve.tensor_tensor(x_sb[:, ts, :], x_sb[:, ts, :], acc[:, ts, :], ALU.add).then_inc(s_res, 1)

        @block.scalar
        def _(act):
            for k in range(2):
                act.wait_ge(s_var2, k + 1)
                act.activation(std[:], vareps[:], ACT.Sqrt).then_inc(s_std2, 1)
            act.wait_ge(s_dif, 1)
            act.activation(exps[:], logits[:], ACT.Exp).then_inc(s_ex, 1)

            def turned():
                act.activation(xsT[:], ps_r[:, 0, :], ACT.Copy).then_inc(s_xsT, 1)

            act.wait_ge(full_x, 1)
            turned()

            def body(q, last_body):
                for word in ORDER:
                    kind, k = word[0], int(word[1])
                    if kind == "B":
                        act.wait_ge(full_hT, BODY * q + k + 1)
                        act.activation(hT[:, k % 2, :], ps_m[:, k % 2, :], ACT.Relu).then_inc(s_hT, 1)
                    if kind == "X" and not last_body:
                        act.wait_ge(full_x, q + 2)
                        turned()

            run_bodies(act, body)
            for c in range(NC):
                act.wait_ge(s_var2, 3 + c)
                act.activation(std[:, 4 * c:4 * c + 4], den[:, 4 * c:4 * c + 4], ACT.Sqrt).then_inc(s_std2, 1)

        @block.tensor
        def _(pe):
            pe.wait_ge(s_small, 32)
            pe.wait_ge(s_x2n, 1)
            for t in range(NT):
                last = pe.transpose(banks[:, t // 4, P * (t % 4):P * (t % 4) + P], xn[:, t, :], identf[:])
                if t % 4 == 3:
                    last.then_inc(s_tr, 1)
            for t in range(NT):
                pe.wait_ge(s_x2T, t // 4 + 1)
                last = pe.matmul(ps_r[:, 0, NE * t:NE * t + NE], xnT[:, P * t:P * t + P], rw[:], start=True, stop=True)
            last.then_inc(s_log, 1)
            pe.wait_ge(s_top1, 1)
            pe.wait_ge(s_c2, 5)
            pe.matmul(ps_m[:, 0, 0:NT * NE], before_b[:], top1_b[:], start=True, stop=False, skip_group_check=True)
            for k in range(1, NT + 1):
                last = pe.matmul(ps_m[:, 0, NE * k:NE * (NT + 1)], ones_b[:], top1_b[:, 0:NE * (NT + 1 - k)],
                                 start=False, stop=k == NT, skip_group_check=True)
            last.then_inc(s_rank, 1)

            def turn(q):
                pe.wait_ge(s_xs, 16 * q + 16)
                for k in range(BODY):
                    last = pe.transpose(ps_r[:, 0, P * k:P * k + P], xs[:, k, :], identf[:])
                last.then_inc(full_x, 1)

            pe.wait_ge(s_expert, 1)
            pe.wait_ge(s_w1, 16)
            pe.wait_ge(s_big, 48)
            turn(0)

            def body(q, last_body):
                es = []
                for word in ORDER:
                    kind, k = word[0], int(word[1])
                    j = BODY * q + k
                    if kind == "A":
                        e = pe.value_load(expert[0:1, bass.ds(j, 1)], min_val=0, max_val=NE - 1)
                        es.append(e)
                        if k == 0:
                            pe.wait_ge(s_xsT, q + 1)
                        pe.matmul(banks[:, k, :], xsT[:, P * k:P * k + P],
                                  w1[:, bass.ds(e, 1), :].rearrange("p e f -> p (e f)"), start=True, stop=True
                                  ).then_inc(full_h, 1)
                    if kind == "B":
                        pe.wait_ge(s_h, j + 1)
                        for f in range(FT):
                            last = pe.transpose(ps_m[:, k % 2, P * f:P * f + P], h[:, k, P * f:P * f + P], identf[:])
                        last.then_inc(full_hT, 1)
                    if kind == "X" and not last_body:
                        turn(q + 1)
                    if kind == "C":
                        pe.wait_ge(s_hT, j + 1)
                        for f in range(FT):
                            last = pe.matmul(ps_r[:, 1, P * k:P * k + P], hT[:, k % 2, P * f:P * f + P],
                                             w2[:, bass.ds(es[k], 1), f, :].rearrange("p e d -> p (e d)"),
                                             start=f == 0, stop=f == FT - 1)
                        if k == BODY - 1:
                            last.then_inc(full_y, 1)

            run_bodies(pe, body)


_INS = ['L0_attn_inputs', 'L0_attn_W_qkv', 'L0_attn_W_out', 'L0_ffn_router_W', 'L0_ffn_router_b', 'L0_ffn_W1',
        'L0_ffn_b1', 'L0_ffn_W2', 'L0_ffn_b2']
_OUTS = [((2, 1024, 128), 'float32')]


def kernel(**inputs):
    import numpy as _np
    import concourse.bacc as _bacc
    from concourse import mybir as _mybir
    from concourse.bass_utils import run_bass_kernel_spmd as _run

    nc = _bacc.Bacc("TRN2", target_bir_lowering=False, num_devices=1)
    arrays, args = {}, []
    for name in _INS:
        a = _np.ascontiguousarray(inputs[name])
        arrays[f"in_{name}_dram"] = a
        args.append(nc.dram_tensor(f"in_{name}_dram", a.shape, _mybir.dt.from_np(a.dtype), kind="ExternalInput").ap())
    for i, (shape, dtype) in enumerate(_OUTS):
        dt = _mybir.dt.from_np(_np.dtype(dtype))
        args.append(nc.dram_tensor(f"out_{i}_dram", shape, dt, kind="ExternalOutput").ap())
    build(nc, *args)
    r = _run(nc, [arrays], core_ids=[0])
    got = tuple(r.results[0][f"out_{i}_dram"] for i in range(len(_OUTS)))
    return got[0]
```

```python
from contextlib import ExitStack

import concourse.bass as bass
from concourse import mybir

F32 = mybir.dt.float32
F32R = mybir.dt.float32r
BF16 = mybir.dt.bfloat16
F16 = mybir.dt.float16
ALU = mybir.AluOpType
ACT = mybir.ActivationFunctionType
AX_X = mybir.AxisListType.X

P = 128
EPS = 1e-5
NEG = -1.0e30


def step_order(r, first, last):
    gone = set()
    if first and r == 0:
        gone |= {"O", "C"}
    if first and r == 1:
        gone |= {"T", "Y"}
    if last and r == 2:
        gone |= {"Q"}
    if last and r == 3:
        gone |= {"M", "R", "V"}
    even = "M0 M1 M2 Q0 M3 M4 Q1 M5 S0 C0 S1 Q2 M6 S2 M7 S3 Q3 M8 S4 S5 O0 S6 M9 S7 S8 M10 S9 M11 O1 B0 R0 S10 S11"
    odd = "M0 M1 T0 T1 M2 M3 Y0 M4 V0 M5 S0 S1 M6 V1 S2 M7 S3 S4 O0 S5 M8 M9 C0 S6 M10 Y1 S7 S8 M11 O1 S9 R0 S10 B0 S11"
    words = (odd if r % 2 else even).split()
    return [(w[0], int(w[1:])) for w in words if w[0] not in gone]


MAX_PIECES = [(i, c, min(512, P * (i + 1) - c)) for i in range(8) for c in range(0, P * (i + 1), 512)][::-1]
NM = len(MAX_PIECES)
SCORE_PIECES = [(j, c, min(512, P * (8 - j) - c)) for j in range(8) for c in range(0, P * (8 - j), 512)]
NS = len(SCORE_PIECES)
PIECES_UPTO = [sum(j < 4 * k + 4 for j, c, w in SCORE_PIECES) for k in range(2)]
RING_S = RING_M = 3

RING_KINDS = "OQVRTY"


def ring_counts(kind, i, r):
    return {
        "O": (8, 2 * (r - 1) + i + 1),
        "Q": (8, 4 * (r // 2 + 1) + i + 1),
        "V": (4, 2 * (r // 2 + 1) + i + 1),
        "R": (4, r + 2),
        "T": (4, 2 * (r // 2 - 1) + i + 1),
        "Y": (4, 2 * (r // 2 - 1) + i + 1),
    }[kind]


def ring_uses(first, last):
    return [((r, k, i), (k, *ring_counts(k, i, r))) for r in range(4) for k, i in step_order(r, first, last)
            if k in RING_KINDS]


def ring_plan():
    pro = [((0, "Q", i), ("Q", 0, i + 1)) for i in range(4)] + [((0, "V", i), ("V", 0, i + 1)) for i in range(2)]
    pro += [((0, "R", 0), ("R", 0, 1))]
    first, mid, last = ring_uses(True, False), ring_uses(False, False), ring_uses(False, True)
    epi = [((4, "O", k), ("O", 8, 6 + k + 1)) for k in range(2)]
    epi += [((5, k, c), (k, 4, 2 + c + 1)) for c in range(2) for k in "TY"]
    back = [(key, (k, a, c - a)) for key, (k, a, c) in mid]
    assert len(mid) % 2 == 0 and len(first) % 2 == 0
    plans = {}
    for name, before, uses, at in (("pro", [], pro, 1), ("first", pro, first, 0), ("mid", back, mid, 0),
                                   ("last", back, last, 0), ("epi", last, epi, len(last))):
        both = before + uses
        n0 = len(before)
        plans[name] = {
            key: ((at + n) % 2, both[n0 + n - 2][1] if n0 + n >= 2 else None) for n, (key, _) in enumerate(uses)
        }
    return plans


def build(nc, x_d, wqkv_d, wout_d, rw_d, rb_d, w1_d, b1_d, w2_d, b2_d, out_d):
    B, L, D = x_d.shape
    HD = wout_d.shape[0]
    DH = 64
    NPAIR = HD // P
    NE, _, F = w1_d.shape
    NT = B * L // P
    IT = L // P
    FT = F // P
    PW = (L + P) * IT // 2
    OFF = [(L + P) * j if j < IT // 2 else (L + P) * (IT - 1 - j) + P * (j + 1) for j in range(IT)]
    VC = DH + 1
    SCALE = DH ** -0.5
    SLOTS = NT + NE
    assert SLOTS % NPAIR == 0 and NE == NPAIR
    assert B == 2 and IT == 8 and D == P and FT == 4 and NE == 8
    RING = ring_plan()

    with ExitStack() as ctx:
        def sb(name, shape, dt=F32):
            return ctx.enter_context(nc.sbuf_tensor(name, shape, dt))

        def sem(name):
            return ctx.enter_context(nc.semaphore(name))

        banks = ctx.enter_context(nc.psum_tensor("banks", [P, 8, 512], F32))
        ps_s, ps_m, ps_r = banks[:, 0:RING_S], banks[:, RING_S:RING_S + RING_M], banks[:, RING_S + RING_M:]

        x_sb = sb("x_sb", [P, NT, D])
        xnT = sb("xnT", [P, NT * P])
        y_acc = sb("y_acc", [P, NT, D])
        identf = sb("identf", [P, P])
        mask_rows = sb("mask_rows", [P, 512])
        stats = sb("stats", [P, NT, 6])
        meanvar = sb("meanvar", [P, NT, 2])
        vareps = sb("vareps", [P, NT])
        std = sb("std", [P, NT])
        rstd = sb("rstd", [P, NT])

        s_x = [sem(f"s_x{b}") for b in range(2)]
        s_const = sem("s_const")
        s_pool = sem("s_pool")
        s_dve = sem("s_dve")
        s_var = sem("s_var")
        s_std = sem("s_std")
        s_xn = sem("s_xn")
        s_xt_full = sem("s_xt_full")
        s_xt = sem("s_xt")

        w_loaded = [sem(f"w_loaded{b}") for b in range(2)]
        s_wout = sem("s_wout")
        full = {k: sem(f"full_{k}") for k in "SMOQVRTY"}
        freed = {k: sem(f"freed_{k}") for k in "OQVRTY"}
        s_hi = sem("s_hi")
        s_q_stacked = sem("s_q_stacked")
        s_k_stacked = sem("s_k_stacked")
        s_v1 = sem("s_v1")
        s_max = sem("s_max")
        s_carry_select = sem("s_carry_select")
        s_carry_max = sem("s_carry_max")
        s_max_all = sem("s_max_all")
        s_mh = sem("s_mh")
        s_m_rows = sem("s_m_rows")
        s_exp = sem("s_exp")
        s_masked = sem("s_masked")
        s_plo = sem("s_plo")
        s_plo_help = sem("s_plo_help")
        s_rec = sem("s_rec")

        RW = 2 * D + 4
        xs_d = nc.dram_tensor("xs_rows", [SLOTS * P, RW], F32, kind="Internal").ap()
        blank = sb("blank", [P, RW])
        weights = sb("weights", [P, NE, F + FT + D])
        s_blank = sem("s_blank")
        s_weights = sem("s_weights")

        main = ExitStack()
        with main:
            def sbm(name, shape, dt=F32):
                return main.enter_context(nc.sbuf_tensor(name, shape, dt))

            W = sbm("W", [P, 2, 3, P])
            wout = sbm("wout", [P, NPAIR * D])
            T1 = sbm("T1", [P, 2, 2, L], F32R)
            T2 = sbm("T2", [P, 2, 2, L], F32R)
            K1 = sbm("K1", [P, 2, 2, L], F32R)
            K2 = sbm("K2", [P, 2, 2, L], F32R)
            q_lo = sbm("q_lo", [P, L], F32R)
            v_hi = sbm("v_hi", [P, 2, IT, 2, VC + 1], BF16)
            v_lo = sbm("v_lo", [P, 2, IT, 2, DH], F16)
            probs = sbm("probs", [P, 2, PW])
            xn = probs[:, 0, 0:NT * D].rearrange("q (t d) -> q t d", d=D)
            probs_lo = sbm("probs_lo", [P, 2, PW], F16)
            junk = sbm("junk", [P, RING_M, 512], BF16)
            mx_half = sbm("mx_half", [P, 2, 2, IT])
            mx = sbm("mx", [P, 2, IT])
            mh = sbm("mh", [IT, 2, P], F32R)
            ml = sbm("ml", [IT, 2, P], F32R)
            rec = sbm("rec", [P, IT])
            o_sb = sbm("o_sb", [P, 2, IT, P])
            oT = sbm("oT", [P, 2, 512])

            probs_hi = probs[:].bitcast(BF16).rearrange("p g (n t) -> p g n t", t=2)[:, :, :, 1]
            OWN = [(0, 64), (64, 128)]
            OTHER = [(64, 128), (0, 64)]

            def w_slice(p):
                return wqkv_d.rearrange("r (t p c) -> r t p c", t=3, p=NPAIR)[:, :, bass.ds(p, 1), :].rearrange(
                    "r t p c -> r t (p c)")

            block = main.enter_context(nc.Block())

            def run_bodies(eng, body):
                body(0, "first")
                with eng.Fori(1, NPAIR - 1) as p:
                    body(p, "mid")
                body(NPAIR - 1, "last")

            def stages(name):
                for r in range(4):
                    for kind, i in step_order(r, name == "first", name == "last"):
                        yield r, kind, i

            @block.sync
            def _(sp):
                for b in range(2):
                    sp.dma_start(x_sb[:, IT * b:IT * b + IT, :], x_d[b].rearrange("(t p) d -> p t d", p=P)
                                 ).then_inc(s_x[b], 16)
                for b in range(2):
                    sp.dma_start(W[:, b], w_slice(0)).then_inc(w_loaded[b], 16)
                sp.dma_start(wout[:].rearrange("r (p n) -> r p n", n=D),
                             wout_d.rearrange("(p r) n -> r p n", r=P)).then_inc(s_wout, 16)

                def stack_q(u, b):
                    sp.wait_ge(freed["Q"], 4 * u + 2)
                    for s in range(2):
                        (o0, o1), (t0, t1) = OWN[s], OTHER[s]
                        sp.dma_start(T1[t0:t1, b, s, :].bitcast(F32), q_lo[o0:o1, :].bitcast(F32)
                                     ).then_inc(s_q_stacked, 16)
                        sp.dma_start(T2[o0:o1, b, s, :].bitcast(F32), T1[o0:o1, b, s, :].bitcast(F32)
                                     ).then_inc(s_q_stacked, 16)

                def stack_k(u, b):
                    sp.wait_ge(s_hi, 4 * u + 4)
                    for s in range(2):
                        (o0, o1), (t0, t1) = OWN[s], OTHER[s]
                        sp.dma_start(K1[t0:t1, b, s, :].bitcast(F32), K1[o0:o1, b, s, :].bitcast(F32)
                                     ).then_inc(s_k_stacked, 16)

                def max_rows(g, b, s):
                    t0 = OTHER[s][0]
                    for n, (part, ready) in enumerate(((mh, s_mh), (ml, freed["R"]))):
                        sp.wait_ge(ready, g + 1)
                        sp.dma_start(T2[t0 + n:t0 + n + 1, b, s, :].bitcast(F32).rearrange(
                            "o (t i) -> o t i", i=P), part[:, s, :].bitcast(F32)).then_inc(s_m_rows, 16)

                stack_q(0, 0)
                stack_k(0, 0)
                max_rows(0, 0, 0)
                sp.wait_ge(s_const, 9)
                sp.dma_start(weights[:, :, F + FT:], b2_d.partition_broadcast(P)).then_inc(s_weights, 16)

                def body(p, name):
                    for r, kind, i in stages(name):
                        u1 = 2 * p + r // 2 + 1
                        b1 = (r // 2 + 1) % 2
                        if r in (0, 2) and (kind, i) == ("S", 0) and name != "last":
                            b = r // 2
                            sp.wait_ge(full["V"], 4 * p + 2 * b + 2)
                            sp.dma_start(W[:, b], w_slice(p + 1)).then_inc(w_loaded[b], 16)
                        if (r, kind, i) == (1, "S", 0):
                            sp.dma_start(weights[:, bass.ds(p, 1), 0:F].rearrange("r e f -> r (e f)"),
                                         w1_d[bass.ds(p, 1)].rearrange("e r f -> r (e f)")).then_inc(s_weights, 16)
                        if (r, kind, i) == (3, "S", 0):
                            sp.dma_start(xs_d.rearrange("(p k q) c -> p q k c", p=NPAIR, q=P)[bass.ds(p, 1)].rearrange(
                                "p q k c -> q (p k) c"), blank[:].unsqueeze(1).to_broadcast([P, SLOTS // NPAIR, RW])
                                         ).then_inc(s_blank, 16)
                        if (kind, i) == ("Q", 1):
                            stack_q(u1, b1)
                        if (kind, i) == ("Q", 3):
                            stack_k(u1, b1)
                        if kind == "R":
                            max_rows(4 * p + r + 1, (r + 1) // 2 % 2, (r + 1) % 2)

                run_bodies(sp, body)

            @block.gpsimd
            def _(pool):
                n = [0]

                def link(ins):
                    n[0] += 1
                    ins.then_inc(s_pool, 1)
                    pool.wait_ge(s_pool, n[0])

                link(pool.memset(identf[:], 0.0))
                pool.affine_select(out=identf[:], in_=identf[:], compare_op=ALU.not_equal, fill=1.0, base=0,
                                   pattern=[[-1, P]], channel_multiplier=1).then_inc(s_const, 1)
                pool.memset(T2[:].bitcast(F32), 0.0).then_inc(s_const, 1)
                pool.memset(y_acc[:], 0.0).then_inc(s_const, 1)
                link(pool.memset(K2[:].bitcast(F32), 0.0))
                for s in range(2):
                    t0 = OTHER[s][0]
                    pool.memset(K2[t0:t0 + 2, :, s, :].bitcast(F32), 1.0).then_inc(s_const, 1)
                    pool.wait_ge(s_const, 4 + s)
                pool.memset(mx_half[:], -3.0e38).then_inc(s_const, 1)
                link(pool.memset(mask_rows[:], 0.0))
                link(pool.memset(blank[:], 0.0))
                pool.memset(blank[:, 2 * D + 1:2 * D + 2], float(NT * P)).then_inc(s_const, 1)
                pool.affine_select(out=mask_rows[:, 512 - P:], in_=mask_rows[:, 512 - P:], compare_op=ALU.is_ge,
                                   fill=NEG, base=0, pattern=[[-1, P]], channel_multiplier=1).then_inc(s_const, 1)
                pool.memset(v_hi[:, :, :, :, DH:], 1.0).then_inc(s_const, 1)

                def p_low(g, s, k, tiles=None):
                    pool.wait_ge(s_exp, NS * g + PIECES_UPTO[k])
                    pool.sem_inc(s_carry_select, 1)
                    if k == 0:
                        blocks = probs[:, s, :].rearrange("q (j c) -> q j c", c=L + P)[:, :, 0:P]
                    else:
                        blocks = probs[:, s, L // 2:].rearrange("q (j c) -> q j c", c=L)[:, :, L // 2:L // 2 + P]
                    pool.affine_select(out=blocks, in_=blocks, compare_op=ALU.is_ge, fill=0.0, base=0,
                                       pattern=[[0, 4], [1, P]], channel_multiplier=-1).then_inc(s_masked, 1)
                    pool.wait_ge(s_masked, 2 * g + k + 1)
                    for j in range(4 * k, 4 * k + 4) if tiles is None else tiles:
                        part = slice(OFF[j], OFF[j] + L - P * j)
                        pool.tensor_tensor(probs_lo[:, s, part], probs[:, s, part], probs_hi[:, s, part],
                                           ALU.subtract).then_inc(s_plo, 1)

                def body(p, name):
                    for r, kind, i in stages(name):
                        if kind == "B":
                            p_low(4 * p + r, r % 2, 0, [2, 3] if name == "last" and r == 3 else None)
                        if kind == "C":
                            p_low(4 * p + r - 1, (r - 1) % 2, 1)

                run_bodies(pool, body)
                p_low(4 * NPAIR - 1, 1, 1, [])

            @block.vector
            def _(dve):
                n = [0]

                def link(ins):
                    n[0] += 1
                    ins.then_inc(s_dve, 1)
                    dve.wait_ge(s_dve, n[0])

                for b in range(2):
                    ts = slice(IT * b, IT * b + IT)
                    dve.wait_ge(s_x[b], 16)
                    for t in range(IT * b, IT * b + IT):
                        last = dve.bn_stats(stats[:, t, :], x_sb[:, t, :])
                    link(last)
                    for t in range(IT * b, IT * b + IT):
                        last = dve.bn_aggr(meanvar[:, t, :], stats[:, t, :])
                    link(last)
                    dve.tensor_scalar(vareps[:, ts], meanvar[:, ts, 1], EPS, None, ALU.add).then_inc(s_var, 1)
                    dve.wait_ge(s_std, b + 1)
                    link(dve.reciprocal(rstd[:, ts], std[:, ts]))
                    for t in range(IT * b, IT * b + IT):
                        dve.tensor_scalar(xn[:, t, :], x_sb[:, t, :], meanvar[:, t, 0:1], rstd[:, t:t + 1],
                                          ALU.subtract, ALU.mult).then_inc(s_xn, 1)

                dve.wait_ge(s_const, 9)

                def q_low(u, b, i, bank):
                    dve.wait_ge(s_hi, 4 * u + i + 1)
                    c = 512 * (i % 2)
                    for s in range(2):
                        o0, o1 = OWN[s]
                        hi = (T1 if i < 2 else K1)[o0:o1, b, s, c:c + 512].bitcast(F32)
                        dst = q_lo[o0:o1, c:c + 512] if i < 2 else K2[o0:o1, b, s, c:c + 512]
                        last = dve.tensor_tensor(dst, ps_r[o0:o1, bank, :], hi, ALU.subtract)
                    last.then_inc(freed["Q"], 1)

                def v_low(u, b, i, bank):
                    dve.wait_ge(s_v1, 2 * u + i + 1)
                    dve.tensor_tensor(v_lo[:, b, 4 * i:4 * i + 4, :, :],
                                      ps_r[:, bank, :].rearrange("p (t s d) -> p t s d", t=4, s=2),
                                      v_hi[:, b, 4 * i:4 * i + 4, :, 0:DH], ALU.subtract).then_inc(freed["V"], 1)

                def row_max(g, s, n):
                    i, c, w = MAX_PIECES[n]
                    dve.wait_ge(full["M"], NM * g + n + 1)
                    dst = mx_half[:, s, c // 512, i:i + 1]
                    if c + w == P * (i + 1):
                        dve.sem_inc(s_carry_max, 1)
                        dve.tensor_tensor_reduce(junk[:, n % RING_M, 0:w], ps_m[:, n % RING_M, 0:w], mask_rows[:, 512 - w:], 1.0,
                                                 -3.0e38, ALU.add, ALU.max, dst).then_inc(s_max, 1)
                    else:
                        dve.tensor_reduce(dst, ps_m[:, n % RING_M, 0:w], AX_X, ALU.max).then_inc(s_max, 1)
                    if n == NM - 1:
                        dve.wait_ge(s_max, NM * g + NM)
                        dve.tensor_tensor(mx[:, s, :], mx_half[:, s, 0, :], mx_half[:, s, 1, :], ALU.max
                                          ).then_inc(s_max_all, 1)

                def max_split(g, s, bank):
                    dve.wait_ge(full["R"], g + 1)
                    dve.tensor_scalar(mh[:, s, :], ps_r[0:IT, bank, 0:P], -1.0, None, ALU.mult).then_inc(s_mh, 1)
                    dve.wait_ge(s_mh, g + 1)
                    dve.scalar_tensor_tensor(ml[:, s, :], ps_r[0:IT, bank, 0:P], -1.0, mh[:, s, :].bitcast(F32),
                                             ALU.mult, ALU.subtract).then_inc(freed["R"], 1)

                def normalise(g, b, s, k, bank):
                    dve.wait_ge(full["O"], 2 * g + k + 1)
                    four = ps_r[:, bank, 0:4 * VC].rearrange("p (t c) -> p t c", t=4)
                    dve.reciprocal(rec[:, 4 * k:4 * k + 4], four[:, :, DH]).then_inc(s_rec, 1)
                    dve.wait_ge(s_rec, 2 * g + k + 1)
                    dve.tensor_tensor(o_sb[:, b, 4 * k:4 * k + 4, DH * s:DH * s + DH], four[:, :, 0:DH],
                                      rec[:, 4 * k:4 * k + 4].unsqueeze(2).to_broadcast([P, 4, DH]),
                                      ALU.mult).then_inc(freed["O"], 1)

                def accumulate(u, b, c, bank):
                    dve.wait_ge(full["Y"], 2 * u + c + 1)
                    ya = y_acc[:, IT * b + 4 * c:IT * b + 4 * c + 4, :]
                    dve.tensor_tensor(ya, ps_r[:, bank, :].rearrange("p (t d) -> p t d", t=4), ya,
                                      ALU.add).then_inc(freed["Y"], 1)

                for i in range(4):
                    q_low(0, 0, i, RING["pro"][(0, "Q", i)][0])
                for i in range(2):
                    v_low(0, 0, i, RING["pro"][(0, "V", i)][0])
                for i in range(NM):
                    row_max(0, 0, i)
                max_split(0, 0, RING["pro"][(0, "R", 0)][0])

                def body(p, name):
                    for r, kind, i in stages(name):
                        g = 4 * p + r
                        u1, b1 = 2 * p + r // 2 + 1, (r // 2 + 1) % 2
                        bank = RING[name][(r, kind, i)][0] if kind in RING_KINDS else None
                        if kind == "M":
                            if i == 0 and not (name == "first" and r == 0):
                                dve.wait_ge(full["R"], g)
                            row_max(g + 1, (r + 1) % 2, i)
                        if kind == "R":
                            if not (name == "first" and r == 0):
                                dve.wait_ge(s_m_rows, 32 * g)
                            max_split(g + 1, (r + 1) % 2, bank)
                        if kind == "O":
                            normalise(g - 1, (r - 1) // 2 % 2, (r - 1) % 2, i, bank)
                        if kind == "Q":
                            if i == 0:
                                dve.wait_ge(s_q_stacked, 64 * u1)
                            q_low(u1, b1, i, bank)
                        if kind == "V":
                            v_low(u1, b1, i, bank)
                        if kind == "Y":
                            accumulate(u1 - 2, b1, i, bank)

                def help_p_low(k, tiles):
                    dve.wait_ge(s_masked, 2 * (4 * NPAIR - 1) + k + 1)
                    for j in tiles:
                        part = slice(OFF[j], OFF[j] + L - P * j)
                        dve.tensor_tensor(probs_lo[:, 1, part], probs[:, 1, part], probs_hi[:, 1, part], ALU.subtract
                                          ).then_inc(s_plo_help, 1)

                run_bodies(dve, body)
                help_p_low(0, [0, 1])
                help_p_low(1, [4, 5, 6, 7])
                for k in range(2):
                    normalise(4 * NPAIR - 1, 1, 1, k, RING["epi"][(4, "O", k)][0])
                for c in range(2):
                    accumulate(2 * NPAIR - 1, 1, c, RING["epi"][(5, "Y", c)][0])

            @block.scalar
            def _(act):
                def tokens_turned(b):
                    for c in range(2 * b, 2 * b + 2):
                        act.wait_ge(s_xt_full, 4 * c + 4)
                        act.activation(xnT[:, 512 * c:512 * c + 512], banks[:, c % 2, :], ACT.Copy).then_inc(s_xt, 1)

                for b in range(2):
                    ts = slice(IT * b, IT * b + IT)
                    act.wait_ge(s_var, b + 1)
                    act.activation(std[:, ts], vareps[:, ts], ACT.Sqrt).then_inc(s_std, 1)
                    if b == 0:
                        tokens_turned(0)

                def q_high(u, b, i, bank):
                    act.wait_ge(full["Q"], 4 * u + i + 1)
                    c = 512 * (i % 2)
                    for s in range(2):
                        o0, o1 = OWN[s]
                        last = act.activation((T1 if i < 2 else K1)[o0:o1, b, s, c:c + 512], ps_r[o0:o1, bank, :],
                                              ACT.Copy)
                    last.then_inc(s_hi, 1)

                def v_high(u, b, i, bank):
                    act.wait_ge(full["V"], 2 * u + i + 1)
                    act.activation(v_hi[:, b, 4 * i:4 * i + 4, :, 0:DH],
                                   ps_r[:, bank, :].rearrange("p (t s d) -> p t s d", t=4, s=2),
                                   ACT.Copy).then_inc(s_v1, 1)

                def exps(g, s, n):
                    j, c, w = SCORE_PIECES[n]
                    act.wait_ge(full["S"], NS * g + n + 1)
                    act.activation(probs[:, s, OFF[j] + c:OFF[j] + c + w], ps_s[:, n % RING_S, 0:w], ACT.Exp,
                                   scale=SCALE).then_inc(s_exp, 1)

                def o_turned(u, c, bank):
                    act.wait_ge(full["T"], 2 * u + c + 1)
                    act.activation(oT[:, c, :], ps_r[:, bank, :], ACT.Copy).then_inc(freed["T"], 1)

                for i in range(4):
                    q_high(0, 0, i, RING["pro"][(0, "Q", i)][0])
                for i in range(2):
                    v_high(0, 0, i, RING["pro"][(0, "V", i)][0])
                tokens_turned(1)

                def body(p, name):
                    for r, kind, i in stages(name):
                        g = 4 * p + r
                        u1, b1 = 2 * p + r // 2 + 1, (r // 2 + 1) % 2
                        bank = RING[name][(r, kind, i)][0] if kind in RING_KINDS else None
                        if kind == "S":
                            if i == 0 and not (name == "first" and r < 2):
                                act.wait_ge(full["O"], 2 * g - 2)
                            exps(g, r % 2, i)
                        if kind == "Q":
                            q_high(u1, b1, i, bank)
                        if kind == "V":
                            v_high(u1, b1, i, bank)
                        if kind == "T":
                            o_turned(u1 - 2, i, bank)

                run_bodies(act, body)
                for c in range(2):
                    o_turned(2 * NPAIR - 1, c, RING["epi"][(5, "T", c)][0])

            @block.tensor
            def _(pe):
                def wait_bank(use, p):
                    if use is not None:
                        kind, a, c = use
                        pe.wait_ge(freed[kind], a * p + c)

                def project(u, b, i, bank):
                    if i == 0:
                        pe.wait_ge(w_loaded[b], 8 * (u - b) + 16)
                    t = i // 2
                    tok = L * b + 512 * (i % 2)
                    pe.matmul(ps_r[:, bank, :], W[:, b, t, :], xnT[:, tok:tok + 512], start=True, stop=True
                              ).then_inc(full["Q"], 1)

                def values(u, b, i, bank):
                    for t in range(4):
                        tok = L * b + P * (4 * i + t)
                        last = pe.matmul(ps_r[:, bank, P * t:P * t + P], xnT[:, tok:tok + P], W[:, b, 2, :],
                                         start=True, stop=True)
                    last.then_inc(full["V"], 1)

                def max_scores(g, u, b, s, n):
                    if n == 0:
                        pe.wait_ge(s_q_stacked, 64 * u + 64)
                        pe.wait_ge(s_k_stacked, 32 * u + 32)
                    i, c, w = MAX_PIECES[n]
                    pe.matmul(ps_m[:, n % RING_M, 0:w], T1[:, b, s, P * i:P * i + P], K1[:, b, s, c:c + w],
                              start=True, stop=True).then_inc(full["M"], 1)

                def max_turned(g, s, bank):
                    pe.wait_ge(s_max_all, g + 1)
                    pe.transpose(ps_r[0:IT, bank, 0:P], mx[:, s, :], identf[:]).then_inc(full["R"], 1)

                def scores(g, b, s, n):
                    if n == 0:
                        pe.wait_ge(s_m_rows, 32 * g + 32)
                    j, c, w = SCORE_PIECES[n]
                    rows = slice(P * j + c, P * j + c + w)
                    pe.matmul(ps_s[:, n % RING_S, 0:w], K1[:, b, s, P * j:P * j + P], T1[:, b, s, rows],
                              start=True, stop=False)
                    pe.matmul(ps_s[:, n % RING_S, 0:w], K2[:, b, s, P * j:P * j + P], T2[:, b, s, rows],
                              start=False, stop=True).then_inc(full["S"], 1)

                def value_products(g, b, s, k, bank, helped=False):
                    if helped:
                        pe.wait_ge(s_plo, 8 * g + 2)
                        pe.wait_ge(s_plo_help, 2 + 4 * k)
                    else:
                        pe.wait_ge(s_plo, 8 * g + 4 * k + 4)
                    for e in range(4):
                        it = 4 * k + e
                        dst = ps_r[:, bank, VC * e:VC * e + VC]
                        for j in range(it + 1):
                            at = OFF[j] + P * (it - j)
                            hi, lo = probs_hi[:, s, at:at + P], probs_lo[:, s, at:at + P]
                            pe.matmul(dst, hi, v_hi[:, b, j, s, 0:VC], start=j == 0, stop=False,
                                      skip_group_check=True)
                            pe.matmul(dst[:, 0:DH], hi, v_lo[:, b, j, s, :], start=False, stop=False,
                                      skip_group_check=True)
                            last = pe.matmul(dst, lo, v_hi[:, b, j, s, 0:VC], start=False, stop=j == it,
                                             skip_group_check=True)
                    last.then_inc(full["O"], 1)

                def turn_outputs(u, b, c, bank):
                    pe.wait_ge(freed["O"], 4 * u + 2 + c + 1)
                    for t in range(4):
                        last = pe.transpose(ps_r[:, bank, P * t:P * t + P], o_sb[:, b, 4 * c + t, :], identf[:])
                    last.then_inc(full["T"], 1)

                def out_project(u, b, c, p, bank):
                    pe.wait_ge(freed["T"], 2 * u + c + 1)
                    for t in range(4):
                        last = pe.matmul(ps_r[:, bank, P * t:P * t + P], oT[:, c, P * t:P * t + P],
                                         wout[:, bass.ts(p, D)], start=True, stop=True)
                    last.then_inc(full["Y"], 1)

                pe.wait_ge(s_const, 1)

                def turn_tokens(b):
                    for t in range(IT * b, IT * b + IT):
                        if t >= IT and t % 4 == 0:
                            pe.wait_ge(s_xt, t // 4 - 1)
                        pe.wait_ge(s_xn, t + 1)
                        pe.transpose(banks[:, t // 4 % 2, P * (t % 4):P * (t % 4) + P], xn[:, t, :], identf[:]
                                     ).then_inc(s_xt_full, 1)

                turn_tokens(0)
                pe.wait_ge(s_xt, 2)
                for i in range(4):
                    bank, use = RING["pro"][(0, "Q", i)]
                    wait_bank(use, 0)
                    project(0, 0, i, bank)
                for i in range(2):
                    bank, use = RING["pro"][(0, "V", i)]
                    wait_bank(use, 0)
                    values(0, 0, i, bank)
                turn_tokens(1)
                pe.wait_ge(s_const, 9)
                for i in range(NM):
                    if i >= RING_M:
                        pe.wait_ge(s_max, i - RING_M + 1)
                    max_scores(0, 0, 0, 0, i)
                bank, use = RING["pro"][(0, "R", 0)]
                wait_bank(use, 0)
                max_turned(0, 0, bank)
                pe.wait_ge(s_wout, 16)
                pe.wait_ge(s_xt, 4)

                def body(p, name):
                    for r, kind, i in stages(name):
                        g = 4 * p + r
                        u1, b1 = 2 * p + r // 2 + 1, (r // 2 + 1) % 2
                        if kind in RING_KINDS:
                            bank, use = RING[name][(r, kind, i)]
                            wait_bank(use, p)
                        if kind == "S":
                            if not (name == "first" and r == 0 and i < RING_S):
                                pe.wait_ge(s_exp, NS * g + i - RING_S + 1)
                            scores(g, (r // 2) % 2, r % 2, i)
                        if kind == "M":
                            pe.wait_ge(s_max, NM * (g + 1) + i - RING_M + 1)
                            max_scores(g + 1, 2 * p + (r + 1) // 2, (r + 1) // 2 % 2, (r + 1) % 2, i)
                        if kind == "R":
                            max_turned(g + 1, (r + 1) % 2, bank)
                        if kind == "O":
                            if i == 0 and (r - 1) % 2 == 0:
                                pe.wait_ge(freed["V"], 2 * (2 * p + (r - 1) // 2) + 2)
                            value_products(g - 1, (r - 1) // 2 % 2, (r - 1) % 2, i, bank)
                        if kind == "Q":
                            project(u1, b1, i, bank)
                        if kind == "V":
                            values(u1, b1, i, bank)
                        if kind == "T":
                            turn_outputs(u1 - 2, b1, i, bank)
                        if kind == "Y":
                            out_project(u1 - 2, b1, i, p - 1 if r == 1 else p, bank)

                run_bodies(pe, body)
                for k in range(2):
                    bank, use = RING["epi"][(4, "O", k)]
                    wait_bank(use, NPAIR - 1)
                    value_products(4 * NPAIR - 1, 1, 1, k, bank, helped=True)
                for c in range(2):
                    bank, use = RING["epi"][(5, "T", c)]
                    wait_bank(use, NPAIR - 1)
                    turn_outputs(2 * NPAIR - 1, 1, c, bank)
                    bank, use = RING["epi"][(5, "Y", c)]
                    wait_bank(use, NPAIR - 1)
                    out_project(2 * NPAIR - 1, 1, c, NPAIR - 1, bank)

        moe(nc, ctx, sb, sem, x_sb, xnT, y_acc, identf, stats, meanvar, vareps, std, rstd, banks, rw_d, rb_d,
            weights, s_weights, b1_d, w2_d, out_d, xs_d, s_blank, SLOTS, NT, D, NE, F, FT)


def moe(nc, ctx, sb, sem, x_sb, xnT, acc, identf, stats, meanvar, vareps, std, rstd, banks, rw_d, rb_d, weights,
        s_weights, b1_d, w2_d, out_d, xs_d, s_blank, SLOTS, NT, D, NE, F, FT):
    BODY = 4
    NB = SLOTS // BODY
    assert NB % 2 == 0 and SLOTS % BODY == 0
    NC = NT // 4
    RW = xs_d.shape[1]
    AUX = RW - D
    WW = F + FT + D
    GATE, NUMBER, SHIFT = D, D + 1, D + 2
    turned_bank, router_bank, rank_bank, b1_bank = 6, 7, 4, 5
    w2 = sb("w2", [P, NE, FT, D])
    rw = sb("rw", [P, NE])
    rb = sb("rb", [P, NE])
    b1_rows = sb("b1_rows", [NE * FT, P])
    rows = sb("rows", [P, NT, RW])
    stats2 = sb("stats2", [P, NT, 6])
    meanvar2 = sb("meanvar2", [P, NT, 2])
    vareps2 = sb("vareps2", [P, NT])
    std2 = sb("std2", [P, NT])
    rstd2 = sb("rstd2", [P, NT])
    offset2 = sb("offset2", [P, NT])
    logits = sb("logits", [P, NT, NE])
    below = sb("below", [P, NT, NE])
    exps = sb("exps", [P, NT, NE])
    top1 = sb("top1", [P, NT, NE])
    top1_b = sb("top1_b", [P, NT * NE], BF16)
    ones_b = sb("ones_b", [P, P], BF16)
    before_b = sb("before_b", [P, P], BF16)
    falling = sb("falling", [P, NE])
    tile_no = sb("tile_no", [P, SLOTS])
    top_logit = sb("top_logit", [P, NT])
    first_top = sb("first_top", [P, NT])
    den = sb("den", [P, NT])
    count_i = sb("count_i", [P, NE], mybir.dt.int32)
    tiles_i = sb("tiles_i", [P, NE], mybir.dt.int32)
    ends = sb("ends", [P, 4, NE + 4])
    start = sb("start", [P, NE])
    place = sb("place", [P, NT, NE])
    slot_f = sb("slot_f", [P, NT])
    slot = sb("slot", [P, NT], mybir.dt.uint32)
    passed = sb("passed", [P, SLOTS, NE])
    expert_f = sb("expert_f", [P, SLOTS])
    expert = sb("expert", [P, SLOTS], mybir.dt.int32)
    xs = sb("xs", [P, BODY, D])
    aux = sb("aux", [P, SLOTS, AUX])
    xsT = sb("xsT", [P, BODY * P])
    w_now = sb("w_now", [P, 2, BODY, WW])
    hT = sb("hT", [P, BODY, F])
    y = sb("y", [P, BODY, D])
    y_stats = sb("y_stats", [P, BODY, 6])
    y_meanvar = sb("y_meanvar", [P, BODY, 2])
    y_var = sb("y_var", [P, 2, BODY])
    eps = sb("eps", [P, 1])
    keep_table = sb("keep_table", [P, 1])
    y_std = sb("y_std", [P, BODY])
    y_scale = sb("y_scale", [P, 2, BODY])
    y_shift = sb("y_shift", [P, 2, BODY])
    done_rows = sb("done_rows", [P, BODY, D])
    number = sb("number", [P, BODY], mybir.dt.uint32)

    s_small = sem("s_small")
    s_w2 = sem("s_w2")
    s_b1 = sem("s_b1")
    s_b1_turned = sem("s_b1_turned")
    s_const2 = sem("s_const2")
    s_chain = sem("s_chain")
    s_chain2 = sem("s_chain2")
    s_var1 = sem("s_var1")
    s_std1 = sem("s_std1")
    s_rstd1 = sem("s_rstd1")
    s_scaled = sem("s_scaled")
    s_z = sem("s_z")
    s_var2 = sem("s_var2")
    s_std2 = sem("s_std2")
    s_offset2 = sem("s_offset2")
    s_x2n = sem("s_x2n")
    s_x2n_last = sem("s_x2n_last")
    s_x2T_last = sem("s_x2T_last")
    s_turned2 = sem("s_turned2")
    s_x2T = sem("s_x2T")
    s_logits = sem("s_logits")
    s_below = sem("s_below")
    s_exps = sem("s_exps")
    s_top1 = sem("s_top1")
    s_rank = sem("s_rank")
    s_slot = sem("s_slot")
    s_expert = sem("s_expert")
    s_scattered = sem("s_scattered")
    s_aux = sem("s_aux")
    s_xs = sem("s_xs")
    full_x = sem("full_x")
    s_xsT = sem("s_xsT")
    w_ready = [[sem(f"w_ready{side}_{k}") for k in range(BODY)] for side in range(2)]
    s_b1_placed = sem("s_b1_placed")
    full_h = sem("full_h")
    s_hT = sem("s_hT")
    full_y = sem("full_y")
    s_y = sem("s_y")
    s_keep = sem("s_keep")
    s_y_var = sem("s_y_var")
    s_y_std = sem("s_y_std")
    s_done = sem("s_done")
    s_carry2 = sem("s_carry2")
    s_carry_stats = sem("s_carry_stats")
    s_put = sem("s_put")
    s_rows_left = sem("s_rows_left")

    def run_bodies(eng, body):
        body(0, 0, 0, True, False)
        with eng.Fori(0, NB // 2 - 1) as m:
            body(2 * m + 1, 1, m, False, False)
            body(2 * m + 2, 0, m + 1, False, False)
        body(NB - 1, 1, NB // 2 - 1, False, True)

    with nc.Block() as block:
        @block.sync
        def _(sp):
            sp.dma_start(rw[:], rw_d).then_inc(s_small, 16)
            sp.dma_start(rb[:], rb_d.partition_broadcast(P)).then_inc(s_small, 16)
            sp.dma_start(b1_rows[:], b1_d.rearrange("e (f q) -> (e f) q", q=P)).then_inc(s_b1, 16)
            sp.dma_start(w2[:], w2_d.rearrange("e (f q) d -> q e f d", q=P)).then_inc(s_w2, 16)

            def fetch(q):
                sp.dma_start(xs[:], xs_d.rearrange("(b k p) d -> b p k d", p=P, k=BODY)[bass.ds(q, 1)].rearrange(
                    "b p k d -> p (b k) d")[:, :, 0:D]).then_inc(s_xs, 16)

            def take_weights(j, side, k):
                e = sp.value_load(expert[0:1, bass.ds(j, 1)], min_val=0, max_val=NE - 1)
                sp.dma_start(w_now[:, side, k, :], weights[:, bass.ds(e, 1), :].rearrange("p e c -> p (e c)")
                             ).then_inc(w_ready[side][k], 16)

            sp.wait_ge(s_expert, 1)
            sp.wait_ge(s_weights, 16 * NE + 16)
            sp.wait_ge(s_b1_placed, 1)
            for side in range(2):
                for k in range(BODY):
                    take_weights(BODY * side + k, side, k)
            sp.wait_ge(s_scattered, 16 * NT)
            fetch(0)
            sp.dma_start(aux[:], xs_d.rearrange("(k p) d -> p k d", p=P)[:, :, D:]).then_inc(s_aux, 16)
            sp.wait_ge(full_x, 1)
            fetch(1)
            with sp.Fori(0, NB // 2 - 1) as m:
                for side in range(2):
                    q = 2 * m + side
                    for k in range(BODY):
                        sp.wait_ge(s_y, BODY * q + k + 1)
                        take_weights(BODY * (q + 2) + k, side, k)
                        if k == 2:
                            sp.wait_ge(full_x, q + 2)
                            fetch(q + 2)
            sp.wait_ge(s_put, 16 * SLOTS)

        @block.gpsimd
        def _(pool):
            pool.iota(falling[:], [[-1, NE]], base=NE, channel_multiplier=0,
                      allow_small_or_imprecise_dtypes=True).then_inc(s_const2, 1)
            pool.iota(tile_no[:], [[1, SLOTS]], base=0, channel_multiplier=0,
                      allow_small_or_imprecise_dtypes=True).then_inc(s_const2, 1)
            pool.iota(rows[:, :, D + NUMBER], [[P, NT]], base=0, channel_multiplier=1,
                      allow_small_or_imprecise_dtypes=True).then_inc(s_const2, 1)
            pool.memset(ends[:], 0.0).then_inc(s_const2, 1)
            pool.memset(rows[:, :, D + SHIFT + 1:], 0.0).then_inc(s_const2, 1)
            pool.memset(eps[:], EPS).then_inc(s_const2, 1)
            pool.memset(ones_b[:], 1.0).then_inc(s_const2, 1)
            pool.wait_ge(s_const2, 7)
            for c in range(NC):
                ts = slice(4 * c, 4 * c + 4)
                z = rows[:, ts, D:2 * D]
                pool.wait_ge(s_rstd1, c + 1)
                pool.tensor_tensor(z, acc[:, ts, :], rstd[:, ts].unsqueeze(2).to_broadcast([P, 4, D]), ALU.mult
                                   ).then_inc(s_scaled, 1)
                pool.wait_ge(s_scaled, c + 1)
                pool.tensor_tensor(z, z, x_sb[:, ts, :], ALU.add).then_inc(s_z, 1)
            pool.affine_select(out=before_b[:], in_=ones_b[:], compare_op=ALU.is_gt, fill=0.0, base=0,
                               pattern=[[1, P]], channel_multiplier=-1).then_inc(s_const2, 1)
            pool.wait_ge(s_blank, 16 * NE)
            pool.wait_ge(s_slot, 1)
            for t in range(NT):
                pool.indirect_dma_start(xs_d, bass.IndirectOffsetOnAxis(ap=slot[:, t:t + 1], axis=0), rows[:, t, :],
                                        None).then_inc(s_scattered, 16)
            out_rows = out_d.rearrange("b l d -> (b l) d")
            pool.sem_inc(s_rows_left, 1)
            with pool.Fori(0, NB) as q:
                pool.wait_ge(s_done, q + 1)
                pool.sem_inc(s_carry2, 1)
                for k in range(BODY):
                    pool.indirect_dma_start(out_rows, bass.IndirectOffsetOnAxis(ap=number[:, k:k + 1], axis=0),
                                            done_rows[:, k, :], None, bounds_check=NT * P - 1, oob_is_err=False
                                            ).then_inc(s_put, 16)
                pool.wait_ge(s_put, 16 * BODY * q + 16 * BODY)
                pool.sem_inc(s_rows_left, 1)

        @block.vector
        def _(dve):
            n = [0]

            def link(ins):
                n[0] += 1
                ins.then_inc(s_chain, 1)
                dve.wait_ge(s_chain, n[0])

            def variance(src, st, mv, ve, s_var, c):
                ts = range(4 * c, 4 * c + 4)
                for t in ts:
                    last = dve.bn_stats(st[:, t, :], src(t))
                link(last)
                for t in ts:
                    last = dve.bn_aggr(mv[:, t, :], st[:, t, :])
                link(last)
                dve.tensor_scalar(ve[:, 4 * c:4 * c + 4], mv[:, 4 * c:4 * c + 4, 1], EPS, None, ALU.add
                                  ).then_inc(s_var, 1)

            def first_norm(c):
                ts = slice(4 * c, 4 * c + 4)
                link(dve.scalar_tensor_tensor(rows[:, ts, D + SHIFT], meanvar[:, ts, 0], -1.0, rstd[:, ts],
                                              ALU.mult, ALU.mult))
                dve.wait_ge(s_z, c + 1)
                variance(lambda t: rows[:, t, D:2 * D], stats2, meanvar2, vareps2, s_var2, c)

            def second_norm(c):
                ts = slice(4 * c, 4 * c + 4)
                dve.wait_ge(s_std2, c + 1)
                link(dve.reciprocal(rstd2[:, ts], std2[:, ts]))
                dve.scalar_tensor_tensor(offset2[:, ts], meanvar2[:, ts, 0], -1.0, rstd2[:, ts], ALU.mult, ALU.mult
                                         ).then_inc(s_offset2, 1)

            def first_rstd(c):
                ts = slice(4 * c, 4 * c + 4)
                dve.wait_ge(s_std1, c + 1)
                dve.reciprocal(rstd[:, ts], std[:, ts]).then_inc(s_rstd1, 1)

            for c in range(NC):
                variance(lambda t: acc[:, t, :], stats, meanvar, vareps, s_var1, c)
                if c > 0:
                    first_rstd(c - 1)
            first_rstd(NC - 1)
            dve.wait_ge(s_rstd1, NC)
            first_norm(0)
            for c in range(1, NC):
                first_norm(c)
                second_norm(c - 1)
            second_norm(NC - 1)
            c = NC - 1
            dve.wait_ge(s_offset2, NC)
            for t in range(4 * c, 4 * c + 4):
                last = dve.tensor_scalar(rows[:, t, 0:D], rows[:, t, D:2 * D], rstd2[:, t:t + 1], offset2[:, t:t + 1],
                                         ALU.mult, ALU.add)
            last.then_inc(s_x2n_last, 1)
            dve.wait_ge(s_turned2, NC)
            dve.tensor_copy(xnT[:, 512 * c:512 * c + 512], banks[:, c, :]).then_inc(s_x2T_last, 1)
            dve.wait_ge(s_b1_turned, 1)
            dve.tensor_copy(weights[:, :, F:F + FT], banks[:, b1_bank, 0:NE * FT].rearrange("p (e f) -> p e f", f=FT)
                            ).then_inc(s_b1_placed, 1)
            dve.wait_ge(s_logits, 1)
            dve.wait_ge(s_small, 32)
            dve.wait_ge(s_const2, 8)

            def per_token(a):
                return a.unsqueeze(2).to_broadcast([P, NT, NE])

            link(dve.tensor_tensor(logits[:], banks[:, router_bank, 0:NT * NE].rearrange("p (t e) -> p t e", e=NE),
                                   rb[:].unsqueeze(1).to_broadcast([P, NT, NE]), ALU.add))
            link(dve.tensor_reduce(top_logit[:], logits[:], AX_X, ALU.max))
            link(dve.tensor_tensor(top1[:], logits[:], per_token(top_logit[:]), ALU.is_ge))
            link(dve.tensor_tensor(top1[:], top1[:], falling[:].unsqueeze(1).to_broadcast([P, NT, NE]), ALU.mult))
            link(dve.tensor_reduce(first_top[:], top1[:], AX_X, ALU.max))
            link(dve.tensor_tensor(top1[:], top1[:], per_token(first_top[:]), ALU.is_equal))
            dve.tensor_copy(top1_b[:], top1[:].rearrange("p t e -> p (t e)")).then_inc(s_top1, 1)
            dve.tensor_tensor(below[:], logits[:], per_token(top_logit[:]), ALU.subtract).then_inc(s_below, 1)
            dve.wait_ge(s_rank, 1)
            link(dve.tensor_scalar(count_i[:], banks[:, rank_bank, NT * NE:NT * NE + NE], float(P - 1), None, ALU.add))
            link(dve.tensor_scalar(tiles_i[:], count_i[:], P.bit_length() - 1, None, ALU.logical_shift_right))
            link(dve.tensor_copy(ends[:, 0, 4:], tiles_i[:]))
            for k in range(3):
                sh = 1 << k
                link(dve.tensor_tensor(ends[:, k + 1, 4:], ends[:, k, 4:], ends[:, k, 4 - sh:4 - sh + NE], ALU.add))
            end = ends[:, 3, 4:]
            link(dve.tensor_tensor(start[:], end, ends[:, 0, 4:], ALU.subtract))
            link(dve.scalar_tensor_tensor(place[:], start[:].unsqueeze(1).to_broadcast([P, NT, NE]), float(P),
                                          banks[:, rank_bank, 0:NT * NE].rearrange("p (t e) -> p t e", e=NE),
                                          ALU.mult, ALU.add))
            link(dve.tensor_tensor(place[:], place[:], top1[:], ALU.mult))
            link(dve.tensor_reduce(slot_f[:], place[:], AX_X, ALU.add))
            dve.wait_ge(s_exps, 1)
            link(dve.tensor_reduce(den[:], exps[:], AX_X, ALU.add))
            dve.reciprocal(rows[:, :, D + GATE], den[:])
            dve.tensor_copy(slot[:], slot_f[:]).then_inc(s_slot, 1)
            link(dve.tensor_tensor(passed[:], tile_no[:].unsqueeze(2).to_broadcast([P, SLOTS, NE]),
                                   end.unsqueeze(1).to_broadcast([P, SLOTS, NE]), ALU.is_ge))
            link(dve.tensor_reduce(expert_f[:], passed[:], AX_X, ALU.add))
            dve.tensor_scalar(expert[:], expert_f[:], float(NE - 1), None, ALU.min).then_inc(s_expert, 1)

            dve.wait_ge(s_aux, 16)

            def finish(q, m):
                gate, shift = aux_column(q, GATE), aux_column(q, SHIFT)
                dve.wait_ge(s_y_std, q + 1)
                at = m
                dve.reciprocal(y_scale[:, 0, :], y_std[:]).then_inc(s_chain2, 1)
                dve.wait_ge(s_chain2, at + 1)
                dve.tensor_tensor(y_scale[:, 1, :], y_scale[:, 0, :], gate, ALU.mult).then_inc(s_chain2, 1)
                dve.wait_ge(s_chain2, at + 2)
                dve.tensor_tensor(y_shift[:, 0, :], y_meanvar[:, :, 0], y_scale[:, 1, :], ALU.mult).then_inc(s_chain2, 1)
                dve.wait_ge(s_chain2, at + 3)
                dve.tensor_tensor(y_shift[:, 1, :], shift, y_shift[:, 0, :], ALU.subtract).then_inc(s_chain2, 1)
                dve.wait_ge(s_chain2, at + 4)
                for k in range(BODY):
                    last = dve.tensor_scalar(y[:, k, :], y[:, k, :], y_scale[:, 1, k:k + 1], y_shift[:, 1, k:k + 1],
                                             ALU.mult, ALU.add)
                last.then_inc(s_chain2, 1)
                dve.wait_ge(s_chain2, at + 5)
                dve.wait_ge(s_rows_left, q + 1)
                dve.tensor_copy(number[:], aux_column(q, NUMBER)).then_inc(s_chain2, 1)
                dve.wait_ge(s_chain2, at + 6)
                dve.tensor_tensor(done_rows[:], y[:], aux_rows(q)[:, :, 0:D], ALU.add).then_inc(s_done, 1)
                dve.wait_ge(s_done, q + 1)

            def aux_rows(q):
                return aux[:, bass.ds(q * BODY, BODY), :]

            def aux_column(q, col):
                return aux_rows(q)[:, :, col]

            LINKS = 9

            def body(q, side, nth, first, last_body):
                base = q * LINKS
                if not first:
                    finish(q - 1, base - LINKS + 3)
                for k in range(BODY):
                    j = BODY * q + k
                    dve.wait_ge(full_y, j + 1)
                    dve.tensor_tensor(y[:, k, :], banks[:, 2 + k, 0:D], w_now[:, side, k, F + FT:], ALU.add
                                      ).then_inc(s_y, 1)
                dve.wait_ge(s_y, BODY * q + BODY)
                for k in range(BODY):
                    last = dve.bn_stats(y_stats[:, k, :], y[:, k, :])
                last.then_inc(s_chain2, 1)
                dve.wait_ge(s_chain2, base + 1)
                dve.sem_inc(s_carry_stats, 1)
                for k in range(BODY):
                    last = dve.bn_aggr(y_meanvar[:, k, :], y_stats[:, k, :])
                last.then_inc(s_chain2, 1)
                dve.wait_ge(s_chain2, base + 2)
                dve.tensor_tensor(y_var[:, 0, :], y_meanvar[:, :, 1], aux_column(q, GATE), ALU.mult).then_inc(s_chain2, 1)
                dve.wait_ge(s_chain2, base + 3)
                dve.tensor_tensor(y_var[:, 1, :], y_var[:, 0, :], aux_column(q, GATE), ALU.mult).then_inc(s_y_var, 1)

            run_bodies(dve, body)
            finish(NB - 1, LINKS * (NB - 1) + 3)

        @block.scalar
        def _(act):
            for c in range(NC):
                act.wait_ge(s_var1, c + 1)
                act.activation(std[:, 4 * c:4 * c + 4], vareps[:, 4 * c:4 * c + 4], ACT.Sqrt).then_inc(s_std1, 1)

            def second_std(c):
                act.wait_ge(s_var2, c + 1)
                act.activation(std2[:, 4 * c:4 * c + 4], vareps2[:, 4 * c:4 * c + 4], ACT.Sqrt).then_inc(s_std2, 1)

            def turned_tokens(c):
                act.wait_ge(s_turned2, c + 1)
                act.activation(xnT[:, 512 * c:512 * c + 512], banks[:, c, :], ACT.Copy).then_inc(s_x2T, 1)

            second_std(0)
            for c in range(NC - 1):
                second_std(c + 1)
                act.wait_ge(s_offset2, c + 1)
                for t in range(4 * c, 4 * c + 4):
                    last = act.activation(rows[:, t, 0:D], rows[:, t, D:2 * D], ACT.Identity,
                                          bias=offset2[:, t:t + 1], scale=rstd2[:, t:t + 1])
                last.then_inc(s_x2n, 1)
                if c > 0:
                    turned_tokens(c - 1)
            turned_tokens(NC - 2)
            act.wait_ge(s_below, 1)
            act.activation(exps[:], below[:], ACT.Exp).then_inc(s_exps, 1)

            def turned():
                act.activation(xsT[:], banks[:, turned_bank, :], ACT.Copy).then_inc(s_xsT, 1)

            def root(q):
                act.wait_ge(s_y_var, q + 1)
                act.activation(y_std[:], y_var[:, 1, :], ACT.Sqrt, bias=eps[:]).then_inc(s_y_std, 1)

            act.wait_ge(full_x, 1)
            turned()

            def body(q, side, nth, first, last_body):
                act.activation(keep_table[:], eps[:], ACT.Sqrt).then_inc(s_keep, 1)
                act.wait_ge(s_keep, q + 1)
                for k in range(BODY):
                    act.wait_ge(full_h, BODY * q + k + 1)
                    for f in range(FT):
                        last = act.activation(hT[:, k, P * f:P * f + P], banks[:, k % 2, P * f:P * f + P], ACT.Relu,
                                              bias=w_now[:, side, k, F + f:F + f + 1])
                    last.then_inc(s_hT, 1)
                    if k == 1 and not first:
                        root(q - 1)
                if not last_body:
                    act.wait_ge(full_x, q + 2)
                    turned()

            run_bodies(act, body)
            root(NB - 1)

        @block.tensor
        def _(pe):
            pe.wait_ge(s_b1, 16)
            pe.transpose(banks[:, b1_bank, 0:NE * FT], b1_rows[:], identf[0:NE * FT, 0:NE * FT]).then_inc(s_b1_turned, 1)
            pe.wait_ge(s_small, 32)

            def route(c):
                if c < NC - 1:
                    pe.wait_ge(s_x2T, c + 1)
                else:
                    pe.wait_ge(s_x2T_last, 1)
                for t in range(4 * c, 4 * c + 4):
                    last = pe.matmul(banks[:, router_bank, NE * t:NE * t + NE], xnT[:, P * t:P * t + P], rw[:],
                                     start=True, stop=True)
                if c == NC - 1:
                    last.then_inc(s_logits, 1)

            for c in range(NC):
                if c < NC - 1:
                    pe.wait_ge(s_x2n, c + 1)
                else:
                    pe.wait_ge(s_x2n_last, 1)
                for t in range(4 * c, 4 * c + 4):
                    last = pe.transpose(banks[:, c, P * (t % 4):P * (t % 4) + P], rows[:, t, 0:D], identf[:])
                last.then_inc(s_turned2, 1)
                if c > 0:
                    route(c - 1)
            route(NC - 1)
            pe.wait_ge(s_top1, 1)
            pe.wait_ge(s_const2, 8)
            pe.matmul(banks[:, rank_bank, 0:NT * NE], before_b[:], top1_b[:], start=True, stop=False,
                      skip_group_check=True)
            for k in range(1, NT + 1):
                last = pe.matmul(banks[:, rank_bank, NE * k:NE * (NT + 1)], ones_b[:], top1_b[:, 0:NE * (NT + 1 - k)],
                                 start=False, stop=k == NT, skip_group_check=True)
            last.then_inc(s_rank, 1)

            def turn(q):
                pe.wait_ge(s_xs, 16 * q + 16)
                for k in range(BODY):
                    last = pe.transpose(banks[:, turned_bank, P * k:P * k + P], xs[:, k, :], identf[:])
                last.then_inc(full_x, 1)

            pe.wait_ge(s_expert, 1)
            pe.wait_ge(s_w2, 16)
            turn(0)

            def body(q, side, nth, first, last_body):
                def hidden(k):
                    j = BODY * q + k
                    pe.wait_ge(w_ready[side][k], 16 * (nth + 1))
                    if k == 0:
                        pe.wait_ge(s_xsT, q + 1)
                    if not (first and k < 2):
                        pe.wait_ge(s_hT, j - 1)
                    for f in range(FT):
                        last = pe.matmul(banks[:, k % 2, P * f:P * f + P], w_now[:, side, k, P * f:P * f + P],
                                         xsT[:, P * k:P * k + P], start=True, stop=True)
                    last.then_inc(full_h, 1)

                def outputs(k):
                    j = BODY * q + k
                    if not first:
                        pe.wait_ge(s_y, j - BODY + 1)
                    e = pe.value_load(expert[0:1, bass.ds(j, 1)], min_val=0, max_val=NE - 1)
                    pe.wait_ge(s_hT, j + 1)
                    for f in range(FT):
                        last = pe.matmul(banks[:, 2 + k, 0:D], hT[:, k, P * f:P * f + P],
                                         w2[:, bass.ds(e, 1), f, :].rearrange("p e d -> p (e d)"),
                                         start=f == 0, stop=f == FT - 1)
                    last.then_inc(full_y, 1)

                hidden(0)
                hidden(1)
                outputs(0)
                hidden(2)
                outputs(1)
                hidden(3)
                if not last_body:
                    turn(q + 1)
                outputs(2)
                outputs(3)

            run_bodies(pe, body)


_INS = ['L0_attn_inputs', 'L0_attn_W_qkv', 'L0_attn_W_out', 'L0_ffn_router_W', 'L0_ffn_router_b', 'L0_ffn_W1',
        'L0_ffn_b1', 'L0_ffn_W2', 'L0_ffn_b2']
_OUTS = [((2, 1024, 128), 'float32')]


def kernel(**inputs):
    import numpy as _np
    import concourse.bacc as _bacc
    from concourse import mybir as _mybir
    from concourse.bass_utils import run_bass_kernel_spmd as _run

    nc = _bacc.Bacc("TRN2", target_bir_lowering=False, num_devices=1)
    arrays, args = {}, []
    for name in _INS:
        a = _np.ascontiguousarray(inputs[name])
        arrays[f"in_{name}_dram"] = a
        args.append(nc.dram_tensor(f"in_{name}_dram", a.shape, _mybir.dt.from_np(a.dtype), kind="ExternalInput").ap())
    for i, (shape, dtype) in enumerate(_OUTS):
        dt = _mybir.dt.from_np(_np.dtype(dtype))
        args.append(nc.dram_tensor(f"out_{i}_dram", shape, dt, kind="ExternalOutput").ap())
    build(nc, *args)
    r = _run(nc, [arrays], core_ids=[0])
    got = tuple(r.results[0][f"out_{i}_dram"] for i in range(len(_OUTS)))
    return got[0]
```
